# Optimizing a Trainium2 kernel written in Bass

```python
import numpy as np
import jax
import jax.numpy as jnp

def _softmax(x, axis=-1):
    return jax.nn.softmax(x, axis=axis)

def _gelu(x):
    return jax.nn.gelu(x, approximate=True)

def _silu(x):
    return jax.nn.silu(x)

def _sigmoid(x):
    return jax.nn.sigmoid(x)

def _layernorm(x, axis=-1, eps=1e-05):
    m = jnp.mean(x, axis=axis, keepdims=True)
    v = jnp.var(x, axis=axis, keepdims=True)
    return (x - m) / jnp.sqrt(v + eps)

def _scatter_add(tgt, idx, src, axis=0):
    return tgt.at[idx].add(src)

def _segment_sum(src, seg, n):
    return jax.ops.segment_sum(src, seg, n)
kernel_name = 'mk_seq_postln_d1_jaxref_r8_b75b42'

def setup_inputs(seed: int=0):
    np.random.seed(seed)
    _w = jnp.asarray

    def _L0_attn_setup():
        import jax, jax.numpy as jnp
        import numpy as np
        H = 8
        R = 2
        D = 128
        DEG = 2
        GATE_OFFSET = 6.906768

        def _power_attention(q, k, v, log_g):
            B, T, hq, d = q.shape
            scale = 1.0 / d ** 0.5
            k = jnp.repeat(k, R, axis=2)
            v = jnp.repeat(v, R, axis=2)
            logG = jnp.cumsum(log_g, axis=1)
            logG = jnp.repeat(logG, R, axis=2)
            logG = jnp.transpose(logG, (0, 2, 1))
            qk = jnp.einsum('bthd,bshd->bhts', q, k) * scale
            a = qk ** DEG
            gate = logG[:, :, :, None] - logG[:, :, None, :]
            causal = jnp.tril(jnp.ones((T, T), dtype=bool))
            a = jnp.where(causal, a * jnp.exp(gate), 0.0)
            norm = jnp.sum(a, axis=-1) + 1e-06
            y = jnp.einsum('bhts,bshd->bthd', a, v)
            y = y / jnp.transpose(norm, (0, 2, 1))[..., None]
            return y
        key = jax.random.key(seed)
        ks = jax.random.split(key, 7)
        B, T, C = (1, 256, 256)
        q_dim = H * R * D
        kv_dim = H * D
        s = 0.02
        return {'hidden_states': jax.random.normal(ks[0], (B, T, C), dtype=jnp.float32), 'Wq': jax.random.normal(ks[1], (C, q_dim), dtype=jnp.float32) * s, 'Wk': jax.random.normal(ks[2], (C, kv_dim), dtype=jnp.float32) * s, 'Wv': jax.random.normal(ks[3], (C, kv_dim), dtype=jnp.float32) * s, 'Wg': jax.random.normal(ks[4], (C, H), dtype=jnp.float32) * s, 'Wc': jax.random.normal(ks[5], (q_dim, C), dtype=jnp.float32) * s, 'bc': jnp.zeros((C,), dtype=jnp.float32)}
    _L0_attn_in = _L0_attn_setup()

    def _L0_ffn_setup():
        import jax, jax.numpy as jnp
        import numpy as np
        TOP_K = 6
        CAP_FACTOR = 2

        def _shared_swiglu(x, wg, wu, wd):
            return jax.nn.silu(x @ wg.T) * (x @ wu.T) @ wd.T
        key = jax.random.key(seed)
        ks = jax.random.split(key, 8)
        B, S, D, E, F, FS = (4, 256, 256, 64, 176, 352)
        scale = jnp.float32(0.02)
        return {'hidden_states': jax.random.normal(ks[0], (B, S, D), jnp.float32), 'gate_w': jax.random.normal(ks[1], (E, D), jnp.float32) * scale, 'w_gate': jax.random.normal(ks[2], (E, F, D), jnp.float32) * scale, 'w_up': jax.random.normal(ks[3], (E, F, D), jnp.float32) * scale, 'w_down': jax.random.normal(ks[4], (E, D, F), jnp.float32) * scale, 'sh_gate': jax.random.normal(ks[5], (FS, D), jnp.float32) * scale, 'sh_up': jax.random.normal(ks[6], (FS, D), jnp.float32) * scale, 'sh_down': jax.random.normal(ks[7], (D, FS), jnp.float32) * scale}
    _L0_ffn_in = _L0_ffn_setup()
    _d = {'L0_attn_hidden_states': _L0_attn_in['hidden_states'], 'L0_attn_Wq': _L0_attn_in['Wq'], 'L0_attn_Wk': _L0_attn_in['Wk'], 'L0_attn_Wv': _L0_attn_in['Wv'], 'L0_attn_Wg': _L0_attn_in['Wg'], 'L0_attn_Wc': _L0_attn_in['Wc'], 'L0_attn_bc': _L0_attn_in['bc'], 'L0_ffn_gate_w': _L0_ffn_in['gate_w'], 'L0_ffn_w_gate': _L0_ffn_in['w_gate'], 'L0_ffn_w_up': _L0_ffn_in['w_up'], 'L0_ffn_w_down': _L0_ffn_in['w_down'], 'L0_ffn_sh_gate': _L0_ffn_in['sh_gate'], 'L0_ffn_sh_up': _L0_ffn_in['sh_up'], 'L0_ffn_sh_down': _L0_ffn_in['sh_down']}
    _x0 = _d['L0_attn_hidden_states']
    _d['L0_attn_hidden_states'] = jax.random.normal(jax.random.fold_in(jax.random.key(seed), 1), (4, 1024, 256), dtype=_x0.dtype)
    del _x0
    return _d

def reference(L0_attn_hidden_states, L0_attn_Wq, L0_attn_Wk, L0_attn_Wv, L0_attn_Wg, L0_attn_Wc, L0_attn_bc, L0_ffn_gate_w, L0_ffn_w_gate, L0_ffn_w_up, L0_ffn_w_down, L0_ffn_sh_gate, L0_ffn_sh_up, L0_ffn_sh_down):

    def _L0_attn_ref(hidden_states, Wq, Wk, Wv, Wg, Wc, bc):
        import jax, jax.numpy as jnp
        import numpy as np
        H = 8
        R = 2
        D = 128
        DEG = 2
        GATE_OFFSET = 6.906768

        def _power_attention(q, k, v, log_g):
            B, T, hq, d = q.shape
            scale = 1.0 / d ** 0.5
            k = jnp.repeat(k, R, axis=2)
            v = jnp.repeat(v, R, axis=2)
            logG = jnp.cumsum(log_g, axis=1)
            logG = jnp.repeat(logG, R, axis=2)
            logG = jnp.transpose(logG, (0, 2, 1))
            qk = jnp.einsum('bthd,bshd->bhts', q, k) * scale
            a = qk ** DEG
            gate = logG[:, :, :, None] - logG[:, :, None, :]
            causal = jnp.tril(jnp.ones((T, T), dtype=bool))
            a = jnp.where(causal, a * jnp.exp(gate), 0.0)
            norm = jnp.sum(a, axis=-1) + 1e-06
            y = jnp.einsum('bhts,bshd->bthd', a, v)
            y = y / jnp.transpose(norm, (0, 2, 1))[..., None]
            return y
        B, T, C = hidden_states.shape
        q = (hidden_states @ Wq).reshape(B, T, H * R, D)
        k = (hidden_states @ Wk).reshape(B, T, H, D)
        v = (hidden_states @ Wv).reshape(B, T, H, D)
        g = hidden_states @ Wg
        log_g = jax.nn.log_sigmoid(GATE_OFFSET + g.astype(jnp.float32))
        y = _power_attention(q, k, v, log_g)
        y = y.reshape(B, T, H * R * D)
        return y @ Wc + bc

    def _L0_ffn_ref(hidden_states, gate_w, w_gate, w_up, w_down, sh_gate, sh_up, sh_down):
        import jax, jax.numpy as jnp
        import numpy as np
        TOP_K = 6
        CAP_FACTOR = 2

        def _shared_swiglu(x, wg, wu, wd):
            return jax.nn.silu(x @ wg.T) * (x @ wu.T) @ wd.T
        B, S, D = hidden_states.shape
        E = gate_w.shape[0]
        x = hidden_states.reshape(-1, D)
        N = x.shape[0]
        A = N * TOP_K
        C = CAP_FACTOR * ((A + E - 1) // E)
        scores = jax.nn.softmax(x @ gate_w.T, axis=-1)
        topk_w, topk_idx = jax.lax.top_k(scores, TOP_K)
        topk_w = topk_w / (topk_w.sum(-1, keepdims=True) + 1e-20)
        flat_e = topk_idx.reshape(-1)
        flat_w = topk_w.reshape(-1)
        order = jnp.argsort(flat_e)
        se = flat_e[order]
        st = order // TOP_K
        sw = flat_w[order]
        counts = jnp.bincount(flat_e, length=E)
        offsets = jnp.cumsum(counts) - counts
        pos = jnp.arange(A) - offsets[se]
        valid = pos < C
        pos_c = jnp.minimum(pos, C - 1)
        buf = jnp.zeros((E, C, D), x.dtype).at[se, pos_c].add(jnp.where(valid[:, None], x[st], jnp.zeros((), x.dtype)))
        g = jnp.einsum('ecd,efd->ecf', buf, w_gate)
        u = jnp.einsum('ecd,efd->ecf', buf, w_up)
        eo = jnp.einsum('ecf,edf->ecd', jax.nn.silu(g) * u, w_down)
        gathered = eo[se, pos_c] * (sw * valid.astype(sw.dtype))[:, None]
        y = jnp.zeros_like(x).at[st].add(gathered).reshape(B, S, D)
        return y + _shared_swiglu(hidden_states, sh_gate, sh_up, sh_down)
    x = L0_attn_hidden_states
    x = _layernorm(x + _L0_attn_ref(x, L0_attn_Wq, L0_attn_Wk, L0_attn_Wv, L0_attn_Wg, L0_attn_Wc, L0_attn_bc), axis=-1)
    x = _layernorm(x + _L0_ffn_ref(x, L0_ffn_gate_w, L0_ffn_w_gate, L0_ffn_w_up, L0_ffn_w_down, L0_ffn_sh_gate, L0_ffn_sh_up, L0_ffn_sh_down), axis=-1)
    return x

_drawn_inputs = setup_inputs


def setup_inputs(seed=0):
    import zlib

    import numpy as np

    out = dict(_drawn_inputs(seed))
    spreads = {'L0_attn_bc': (0.0, 0.1)}
    factors = {'L0_attn_Wg': 8.0,
     'L0_ffn_gate_w': 8.0,
     'L0_ffn_w_gate': 8.0,
     'L0_ffn_w_up': 8.0,
     'L0_ffn_w_down': 8.0,
     'L0_ffn_sh_gate': 2.896,
     'L0_ffn_sh_up': 2.859,
     'L0_ffn_sh_down': 2.858}
    for name, (base, spread) in spreads.items():
        noise = np.random.default_rng([zlib.crc32(name.encode()), seed]).standard_normal(out[name].shape)
        drawn = base * np.exp(spread * noise) if base else spread * noise
        out[name] = jnp.asarray(drawn.astype(out[name].dtype))
    for name, factor in factors.items():
        out[name] = (out[name] * factor).astype(out[name].dtype)
    return out
```

```python
from contextlib import ExitStack
import math

import concourse.bass as bass
from concourse import mybir

F32 = mybir.dt.float32
F32R = mybir.dt.float32r
BF16 = mybir.dt.bfloat16
I32 = mybir.dt.int32
U32 = mybir.dt.uint32
ALU = mybir.AluOpType
ACT = mybir.ActivationFunctionType
AX = mybir.AxisListType

P = 128
B, T, C = 4, 1024, 256
H, R, D = 8, 2, 128
E, F, FS, TOPK, CAP_FACTOR = 64, 176, 352, 6, 2
N = B * T
CC = C // P
TILES = T // P
GROUP = 2 * P
NG = T // GROUP
GATE_OFFSET = 6.906768
SCALE = 1.0 / D ** 0.5
NORM_EPS = 1e-6
LN_EPS = 1e-5
TOPK_EPS = 1e-20
CAP = CAP_FACTOR * ((N * TOPK + E - 1) // E)
CT = CAP // P
VW = D + 2
NOWHERE = 1 << 20
NEG = -1e30
FB = F - P
FBO = 64
GU = 2 * P + FBO + FB
ROW = C + E + 4
TOKEN_COL = C + E
NX = E + FS // F
TOKC = 512

OQ, OK, OV, OC = 0, CC * R * D, CC * (R + 1) * D, CC * (R + 2) * D

K_ID, K_TRI, K_STRICT, K_MASK, K_BASE, K_IOTA, K_END = 0, 128, 256, 384, 640, 704, 768


class Signal:

    def __init__(self, sem, step):
        self.sem, self.step, self.count = sem, step, 0


class Queue:

    def __init__(self):
        self.items, self.reached = [], {}

    def put(self, issue, needs=(), tells=None):
        waits = []
        for sig, value in needs:
            if self.reached.get(sig, 0) < value:
                self.reached[sig] = value
                waits.append((sig.sem, value))
        if tells is not None:
            tells.count += tells.step
        self.items.append((waits, issue, tells))
        return [(tells, tells.count)] if tells is not None else []

    def emit(self, eng):
        for waits, issue, tells in self.items:
            for sem, value in waits:
                eng.wait_ge(sem, value)
            ins = issue(eng)
            if tells is not None:
                ins.then_inc(tells.sem, tells.step)


def f32(ap):
    return ap.bitcast(F32)


def build(nc, xT, x, wall, wg, gw, bc, wgu, wdn, table, out):
    qkv_flat = wall.shape[2]
    slots = nc.dram_tensor("slots", [E * CAP, ROW], F32).ap()
    y_dram = nc.dram_tensor("y_dram", [N + CAP, C], F32).ap()
    x1_dram = nc.dram_tensor("x1_dram", [N, C], F32).ap()
    x1t_dram = nc.dram_tensor("x1t_dram", [2, P, CC, N], F32).ap()
    decay_dram = nc.dram_tensor("decay_dram", [B, H, T], F32).ap()

    with ExitStack() as ctx:
        def signal(name, step=1):
            return Signal(ctx.enter_context(nc.semaphore(name)), step)

        pe, act, dve, pool, sp = Queue(), Queue(), Queue(), Queue(), Queue()

        def sb(stack, name, shape, dt=F32):
            return stack.enter_context(nc.sbuf_tensor(name, shape, dt))

        bank = [ctx.enter_context(nc.psum_tensor(f"bank{i}", [P, 512], F32)) for i in range(8)]

        tab = sb(ctx, "tab", [P, K_END])
        ones = sb(ctx, "ones", [P, P])
        gw_hi = sb(ctx, "gw_hi", [P, CC, E], F32R)
        gw_lo = sb(ctx, "gw_lo", [P, CC, E], F32R)
        strict_bf = sb(ctx, "strict_bf", [P, P], BF16)
        ones_bf = sb(ctx, "ones_bf", [P, P], BF16)
        ident = tab[:, K_ID:K_ID + P]
        tri = tab[:, K_TRI:K_TRI + P]
        mask = tab[:, K_MASK:K_MASK + GROUP]
        acc = [sb(ctx, f"acc{i}", [P, TILES, C]) for i in range(2)]
        rows = sb(ctx, "rows", [P, TILES, ROW])
        x1t_hi = sb(ctx, "x1t_hi", [P, CC, GROUP], F32R)
        x1t_lo = sb(ctx, "x1t_lo", [P, CC, GROUP], F32R)
        stats = sb(ctx, "stats", [P, TILES, 6])
        mv = sb(ctx, "mv", [P, TILES, 2])
        std = sb(ctx, "std", [P, TILES])
        rstd = sb(ctx, "rstd", [P, TILES])
        row_max = sb(ctx, "row_max", [P, TILES])
        row_sum = sb(ctx, "row_sum", [P, TILES])
        row_rec = sb(ctx, "row_rec", [P, TILES])
        top_sum = sb(ctx, "top_sum", [P, TILES])
        top_rec = sb(ctx, "top_rec", [P, TILES])
        shifted = sb(ctx, "shifted", [P, TILES, E])
        scores = sb(ctx, "scores", [P, TILES, E])
        top8 = sb(ctx, "top8", [P, TILES, 8])
        top8_at = sb(ctx, "top8_at", [P, TILES, 8], U32)
        chosen_at = sb(ctx, "chosen_at", [P, TILES, TOPK])
        onehot = sb(ctx, "onehot", [P, TILES // 4 * TOPK, E])
        chosen = sb(ctx, "chosen", [P, TILES, E])
        chosen_bf = sb(ctx, "chosen_bf", [P, TILES, E], BF16)
        taken = sb(ctx, "taken", [P, E])
        slot_of = sb(ctx, "slot_of", [P, TILES, E])
        over = shifted
        slot_f = sb(ctx, "slot_f", [P, TILES, TOPK])
        slot_u = sb(ctx, "slot_u", [P, TILES, TOPK], U32)

        s_const = signal("s_const", 16)
        s_ones = signal("s_ones")
        s_tab = signal("s_tab")
        s_xt_in = signal("s_xt_in", 16)
        s_xt_hi, s_xt_lo = signal("s_xt_hi"), signal("s_xt_lo")
        s_acc_in = [signal(f"s_acc_in{i}", 16) for i in range(2)]
        s_acc0 = signal("s_acc0")
        s_w_in = signal("s_w_in", 16)
        s_w_split = signal("s_w_split")
        s_misc = signal("s_misc")
        s_gate_dve, s_gate_act = signal("s_gate_dve"), signal("s_gate_act")
        s_decay_out = signal("s_decay_out", 16)
        s_decay_in = [signal(f"s_decay_in{i}", 16) for i in range(2)]
        s_mask_dve, s_mask_act = signal("s_mask_dve"), signal("s_mask_act")
        s_qkv_hi, s_qkv_lo = signal("s_qkv_hi"), signal("s_qkv_lo")
        s_scores, s_av = signal("s_scores"), signal("s_av")
        s_sq, s_a32, s_a_hi, s_a_lo = signal("s_sq"), signal("s_a32"), signal("s_a_hi"), signal("s_a_lo")
        s_a_hi_pool = signal("s_a_hi_pool")
        s_off, s_num, s_y = signal("s_off"), signal("s_num"), signal("s_y")
        s_num_act = signal("s_num_act")
        s_yt_hi, s_yt_lo = signal("s_yt_hi"), signal("s_yt_lo")
        s_acc = signal("s_acc")
        s_ln, s_ln_act = signal("s_ln"), signal("s_ln_act")
        s_rows_pool = signal("s_rows_pool")
        s_x1t_hi, s_x1t_lo = signal("s_x1t_hi"), signal("s_x1t_lo")
        s_x1_out = signal("s_x1_out", 16)
        s_x1t_out = signal("s_x1t_out", 16)
        s_route, s_route_act = signal("s_route"), signal("s_route_act")
        s_init = signal("s_init")
        s_slots0 = signal("s_slots0", 16)
        s_scatter = signal("s_scatter", 16)

        misc = {"next": 0, "free": [[], []]}

        def take_misc():
            i = misc["next"]
            misc["next"] = 1 - i
            return i, bank[6 + i], misc["free"][i]

        def three_passes(put_mm, a_hi, a_lo, b_hi, b_lo):
            put_mm(a_hi, b_hi)
            put_mm(a_hi, b_lo)
            put_mm(a_lo, b_hi)

        def product(dst, terms, needs, tells, first=True, last=True):
            mms = []
            for a_hi, a_lo, b_hi, b_lo in terms:
                three_passes(lambda a, b: mms.append((a, b)), a_hi, a_lo, b_hi, b_lo)
            done = []
            for i, (a, b) in enumerate(mms):
                start, stop = first and i == 0, last and i == len(mms) - 1
                done = pe.put(lambda e, a=a, b=b, start=start, stop=stop: e.matmul(
                    dst, a, b, start=start, stop=stop, skip_group_check=True),
                    needs if i == 0 else (), tells if i == len(mms) - 1 else None)
            return done

        sp.put(lambda e: e.dma_start(tab[:, :], table), (), s_const)
        tok = {}
        with ExitStack() as att:
            xt_raw = sb(att, "xt_raw", [P, CC, T // 2])
            xt_hi = sb(att, "xt_hi", [P, CC, T], F32R)
            xt_lo = sb(att, "xt_lo", [P, CC, T], F32R)
            w_raw = sb(att, "w_raw", [P, qkv_flat])
            w_hi = sb(att, "w_hi", [P, OC], F32R)
            w_lo = sb(att, "w_lo", [P, OC], F32R)
            wc_hi = [sb(att, f"wc_hi{i}", [P, R, C], F32R) for i in range(2)]
            wc_lo = [sb(att, f"wc_lo{i}", [P, R, C], F32R) for i in range(2)]
            q_hi = [sb(att, f"q_hi{i}", [P, R, T], F32R) for i in range(2)]
            q_lo = [sb(att, f"q_lo{i}", [P, R, T], F32R) for i in range(2)]
            k_hi = [sb(att, f"k_hi{i}", [P, T], F32R) for i in range(2)]
            k_lo = [sb(att, f"k_lo{i}", [P, T], F32R) for i in range(2)]
            v_hi = [sb(att, f"v_hi{i}", [P, TILES, VW], F32R) for i in range(2)]
            v_lo = [sb(att, f"v_lo{i}", [P, TILES, VW], F32R) for i in range(2)]
            wg_raw = sb(att, "wg_raw", [P, CC, H])
            wg_hi = sb(att, "wg_hi", [P, CC, H], F32R)
            wg_lo = sb(att, "wg_lo", [P, CC, H], F32R)
            gw_raw = sb(att, "gw_raw", [P, CC, E])
            bc_all = sb(att, "bc_all", [P, C])
            zg = sb(att, "zg", [P, TILES, H])
            zn = sb(att, "zn", [P, TILES, H])
            log_g = sb(att, "log_g", [P, TILES, H])
            local = [sb(att, f"local{i}", [P, TILES, H]) for i in range(2)]
            f_t = [sb(att, f"f_t{i}", [P, TILES, H]) for i in range(2)]
            ref = sb(att, "ref", [P, NG, H])
            whole = sb(att, "whole", [P, TILES, H])
            c_arg = sb(att, "c_arg", [P, NG * (NG - 1), H])
            c_s = [sb(att, f"c_s{i}", [P, NG * (NG - 1), H]) for i in range(2)]
            decay_rows = sb(att, "decay_rows", [H, T])
            decay_all = sb(att, "decay_all", [P, T])
            em = [sb(att, f"em{i}", [P, NG, GROUP + P]) for i in range(2)]
            ln_scale2 = sb(att, "ln_scale2", [P, 1])
            ln_scale = sb(att, "ln_scale", [P, 1])
            a32 = [sb(att, f"a32_{i}", [P, R, GROUP]) for i in range(2)]
            a_hi = [sb(att, f"a_hi{i}", [P, R, GROUP], F32R) for i in range(3)]
            a_lo = [sb(att, f"a_lo{i}", [P, R, GROUP], F32R) for i in range(3)]
            num = sb(att, "num", [P, 2, R, VW])
            offs = sb(att, "offs", [P, 2, R, VW])
            nrm = sb(att, "nrm", [P, 2, R])
            rec = sb(att, "rec", [P, 2, R])
            y_n = sb(att, "y_n", [P, 2, R, D])
            yt_hi = sb(att, "yt_hi", [P, R, GROUP], F32R)
            yt_lo = sb(att, "yt_lo", [P, R, GROUP], F32R)
            slot0 = acc[1][:, :, :].rearrange("p j c -> p (j c)")[:, 0:CT * ROW].rearrange("p (j c) -> p j c", c=ROW)

            sp.put(lambda e: e.dma_start(wg_raw[:, :, :], wg), (), s_const)
            sp.put(lambda e: e.dma_start(gw_raw[:, :, :], gw), (), s_const)
            const_in = sp.put(lambda e: e.dma_start(bc_all[:, :], bc.partition_broadcast(P)), (), s_const)
            pool.put(lambda e: e.memset(ones[:, :], 1.0), (), s_ones)
            pool.put(lambda e: e.memset(ones_bf[:, :], 1.0), (), s_ones)
            pool.put(lambda e: e.memset(taken[:, :], 0.0), (), s_ones)
            pool.put(lambda e: e.memset(rows[:, :, TOKEN_COL + 1:ROW], 0.0), (), s_ones)
            pool.put(lambda e: e.memset(ln_scale2[:, :], 2.0 * math.log(SCALE)), (), s_ones)
            pool.put(lambda e: e.memset(ln_scale[:, :], math.log(SCALE)), (), s_ones)
            pool.put(lambda e: e.memset(slot0[:, :, 0:TOKEN_COL], 0.0), (), s_init)
            pool.put(lambda e: e.memset(slot0[:, :, TOKEN_COL + 1:ROW], 0.0), (), s_init)
            slot0_ready = pool.put(lambda e: e.iota(slot0[:, :, TOKEN_COL].bitcast(I32), pattern=[[P, CT]], base=N,
                                                    channel_multiplier=1), (), s_init)
            for i in range(2):
                dve.put(lambda e, i=i: e.memset(f32(v_hi[i][:, :, D:D + 1]), 1.0), (), s_tab)
                dve.put(lambda e, i=i: e.memset(f32(v_hi[i][:, :, D + 1:VW]), 0.0), (), s_tab)
                dve.put(lambda e, i=i: e.memset(f32(v_lo[i][:, :, D:VW]), 0.0), (), s_tab)
            ones_ready = [(s_ones, s_ones.count)]
            dve.put(lambda e: e.tensor_copy(strict_bf[:, :], tab[:, K_STRICT:K_STRICT + P]), const_in, s_tab)
            dve.put(lambda e: e.tensor_copy(wg_hi[:, :, :], wg_raw[:, :, :]), (), s_tab)
            t = dve.put(lambda e: e.tensor_copy(gw_hi[:, :, :], gw_raw[:, :, :]), (), s_tab)
            dve.put(lambda e: e.tensor_tensor(wg_lo[:, :, :], wg_raw[:, :, :], f32(wg_hi[:, :, :]), ALU.subtract), t, s_tab)
            tab_ready = dve.put(lambda e: e.tensor_tensor(gw_lo[:, :, :], gw_raw[:, :, :], f32(gw_hi[:, :, :]),
                                                          ALU.subtract), (), s_tab)

            def prepare_batch(b):
                i = b % 2
                for half in range(2):
                    hs = slice(half * T // 2, (half + 1) * T // 2)
                    loaded = sp.put(lambda e, half=half: e.dma_start(
                        xt_raw[:, :, :], xT[:, :, b * T + half * T // 2:b * T + (half + 1) * T // 2]),
                        tok.get("xt_lo", []), s_xt_in)
                    hi = act.put(lambda e, hs=hs: e.activation(xt_hi[:, :, hs], xt_raw[:, :, :], ACT.Copy),
                                 loaded + tok.get("qkv_mm", []), s_xt_hi)
                    lo = dve.put(lambda e, hs=hs: e.tensor_tensor(xt_lo[:, :, hs], xt_raw[:, :, :],
                                                                  f32(xt_hi[:, :, hs]), ALU.subtract), hi, s_xt_lo)
                    tok["xt_lo"] = lo
                tok["xt"] = hi + lo
                got = sp.put(lambda e: e.dma_start(acc[i][:, :, :], x[b * T:(b + 1) * T, :].rearrange(
                    "(j p) c -> p j c", p=P)), tok.get(("ln", b - 2), []) + ([(s_slots0, s_slots0.count)] if b == 1 else []),
                             s_acc_in[i])
                tok["acc0", b] = pool.put(lambda e: e.tensor_tensor(
                    acc[i][:, :, :], acc[i][:, :, :], bc_all[:, :].unsqueeze(1).to_broadcast([P, TILES, C]), ALU.add),
                    got + const_in, s_acc0)

            def gates(b):
                i = b % 2
                m, ps, free = take_misc()
                g_ps = ps[:, 0:TILES * H].rearrange("p (j h) -> p j h", h=H)
                for j in range(TILES):
                    mm = product(g_ps[:, j, :], [(xt_hi[:, c, j * P:(j + 1) * P], xt_lo[:, c, j * P:(j + 1) * P],
                                                  wg_hi[:, c, :], wg_lo[:, c, :]) for c in range(CC)],
                                 tok["xt"] + tab_ready + free, s_misc if j == TILES - 1 else None)
                g = s_gate_dve
                t = dve.put(lambda e: e.tensor_scalar(zg[:, :, :], g_ps, GATE_OFFSET, None, ALU.add),
                            mm, g)
                misc["free"][m] = t
                t = dve.put(lambda e: e.scalar_tensor_tensor(out=zn[:, :, :], in0=zg[:, :, :], scalar=-1.0,
                                                             in1=zg[:, :, :], op0=ALU.mult, op1=ALU.min), t, g)
                t = act.put(lambda e: e.activation(zn[:, :, :], zn[:, :, :], ACT.Exp), t, s_gate_act)
                t = act.put(lambda e: e.activation(zn[:, :, :], zn[:, :, :], ACT.Ln, bias=ones[:, 0:1]),
                            t + ones_ready, s_gate_act)
                t = dve.put(lambda e: e.scalar_tensor_tensor(out=log_g[:, :, :], in0=zg[:, :, :], scalar=0.0,
                                                             in1=zn[:, :, :], op0=ALU.min, op1=ALU.subtract), t, g)
                m, ps, free = take_misc()
                loc = ps[:, 0:TILES * H].rearrange("p (j h) -> p j h", h=H)
                pair = ps[:, 0:TILES * H].rearrange("p (g k h) -> p g k h", k=2, h=H)
                lg_pair = log_g[:, :, :].rearrange("p (g k) h -> p g k h", k=2)
                tot = ps[:, TILES * H:2 * TILES * H].rearrange("p (g k h) -> p g k h", k=2, h=H)
                pe.put(lambda e: e.matmul(loc, tri, log_g[:, :, :], start=True, stop=False, skip_group_check=True),
                       t + free)
                pe.put(lambda e: e.matmul(pair[:, :, 1, :], ones[:, :], lg_pair[:, :, 0, :], start=False, stop=True,
                                          skip_group_check=True))
                mm = pe.put(lambda e: e.matmul(tot, ones[:, :], log_g[:, :, :], start=False, stop=True,
                                               skip_group_check=True), (), s_misc)
                heads_past = tok.get(("heads", b - 2), [])
                dve.put(lambda e: e.tensor_copy(local[i][:, :, :], loc), mm + heads_past, g)
                dve.put(lambda e: e.memset(ref[:, 0, :], 0.0), (), g)
                t = dve.put(lambda e: e.tensor_tensor(ref[:, 1, :], tot[:, 0, 0, :], ref[:, 0, :], ALU.add),
                            [(g, g.count)], g)
                t = dve.put(lambda e: e.tensor_tensor(ref[:, 1, :], tot[:, 0, 1, :], ref[:, 1, :], ALU.add), t, g)
                for k in range(2, NG):
                    t = dve.put(lambda e, k=k: e.tensor_tensor(ref[:, k, :], tot[:, k - 1, 0, :], ref[:, k - 1, :],
                                                               ALU.add), t, g)
                    t = dve.put(lambda e, k=k: e.tensor_tensor(ref[:, k, :], tot[:, k - 1, 1, :], ref[:, k, :],
                                                               ALU.add), t, g)
                misc["free"][m] = t
                t = dve.put(lambda e: e.tensor_tensor(
                    whole[:, :, :].rearrange("p (g k) h -> p g k h", k=2),
                    local[i][:, :, :].rearrange("p (g k) h -> p g k h", k=2),
                    ref[:, :, :].unsqueeze(2).to_broadcast([P, NG, 2, H]), ALU.add), t, g)
                for k in range(1, NG):
                    t = dve.put(lambda e, k=k: e.tensor_tensor(
                        c_arg[:, k * (k - 1):k * (k + 1), :],
                        ref[:, k, :].unsqueeze(1).to_broadcast([P, 2 * k, H]), whole[:, 0:2 * k, :],
                        ALU.subtract), t + [(s_gate_act, s_gate_act.count)], g)
                t = act.put(lambda e: e.activation(c_s[i][:, :, :], c_arg[:, :, :], ACT.Exp,
                                                   bias=ln_scale[:, :], scale=0.5), t + heads_past, s_gate_act)
                t = act.put(lambda e: e.activation(f_t[i][:, :, :], local[i][:, :, :], ACT.Exp), (), s_gate_act)
                for half in range(2):
                    m, ps, free = take_misc()
                    gs = range(half * NG // 2, (half + 1) * NG // 2)
                    for n, k in enumerate(gs):
                        o = ps[0:H, n * GROUP:(n + 1) * GROUP]
                        pe.put(lambda e, o=o, k=k, n=n: e.matmul(o[:, 0:P], log_g[:, 2 * k, :], tri, start=(n == 0),
                                                                 stop=False, skip_group_check=True), free)
                        pe.put(lambda e, o=o, k=k: e.matmul(o[:, P:GROUP], log_g[:, 2 * k, :], ones[:, :], start=False,
                                                            stop=False, skip_group_check=True))
                        mm = pe.put(lambda e, o=o, k=k: e.matmul(o[:, P:GROUP], log_g[:, 2 * k + 1, :], tri,
                                                                 start=False, stop=True, skip_group_check=True),
                                    (), s_misc if n == 1 else None)
                    t = dve.put(lambda e, ps=ps, half=half: e.tensor_copy(
                        decay_rows[:, half * 512:(half + 1) * 512], ps[0:H, :]), mm + tok.get("decay_out", []), g)
                    misc["free"][m] = t
                tok["gates", b] = [(s_gate_dve, s_gate_dve.count), (s_gate_act, s_gate_act.count)]
                tok["log_g_read"] = mm
                tok["decay_out"] = sp.put(lambda e: e.dma_start(decay_dram[b], decay_rows[:, :]), t, s_decay_out)
                tok["decay_out", b] = tok["decay_out"]

            def decay_matrices(n):
                b, h = divmod(n, H)
                i = n % 2
                loaded = sp.put(lambda e: e.dma_start(decay_all[:, :], decay_dram[b, h:h + 1, :].to_broadcast([P, T])),
                                tok["decay_out", b] + tok.get(("em_arg", n - 1), []), s_decay_in[i])
                bi = b % 2
                free = tok.get(("head_a32", n - 2), [])
                for k in range(NG):
                    dve.put(lambda e, k=k: e.scalar_tensor_tensor(
                        out=em[i][:, k, 0:GROUP], in0=decay_all[:, k * GROUP:(k + 1) * GROUP],
                        scalar=local[bi][:, 2 * k, h:h + 1], in1=mask, op0=ALU.subtract, op1=ALU.min),
                        loaded + free + tok["gates", b], s_mask_dve)
                    t = dve.put(lambda e, k=k: e.scalar_tensor_tensor(
                        out=em[i][:, k, GROUP:GROUP + P], in0=decay_all[:, k * GROUP + P:(k + 1) * GROUP],
                        scalar=local[bi][:, 2 * k + 1, h:h + 1], in1=mask[:, 0:P], op0=ALU.subtract, op1=ALU.min),
                        (), s_mask_dve)
                tok["em_arg", n] = t
                tok["em", n] = act.put(lambda e: e.activation(em[i][:, :, :], em[i][:, :, :], ACT.Exp,
                                                              bias=ln_scale2[:, :]), t, s_mask_act)

            def load_weights(n):
                h, i = n % H, n % 2
                got = sp.put(lambda e: e.dma_start(w_raw[:, :], wall[h]), tok.get("w_split", []), s_w_in)
                pool.put(lambda e: e.tensor_copy(w_hi[:, :], w_raw[:, 0:OC]), got + tok.get("qkv_mm", []), s_w_split)
                raw_c = w_raw[:, OC:].rearrange("p (r m) -> p r m", r=R)
                hi = pool.put(lambda e: e.tensor_copy(wc_hi[i][:, :, :], raw_c), tok.get(("proj", n - 2), []), s_w_split)
                pool.put(lambda e: e.tensor_tensor(w_lo[:, :], w_raw[:, 0:OC], f32(w_hi[:, :]), ALU.subtract), hi,
                         s_w_split)
                tok["w_split"] = tok["w", n] = pool.put(lambda e: e.tensor_tensor(
                    wc_lo[i][:, :, :], raw_c, f32(wc_hi[i][:, :, :]), ALU.subtract), (), s_w_split)

            def weights(hi):
                w = w_hi if hi else w_lo
                return [w[:, o:z].rearrange("p (c m) -> p c m", c=CC) for o, z in ((OQ, OK), (OK, OV), (OV, OC))]

            def qkv_tasks(n):
                i = n % 2
                hi, lo = weights(True), weights(False)
                tasks = []

                def split(ps, m, mm, dst_hi, dst_lo, src):
                    t = act.put(lambda e: e.activation(dst_hi, src, ACT.Copy), mm + tok.get(("av", n - 2), []), s_qkv_hi)
                    t2 = dve.put(lambda e: e.tensor_tensor(dst_lo, src, f32(dst_hi), ALU.subtract), mm + t, s_qkv_lo)
                    misc["free"][m] = t + t2
                    tok["qkv", n] = t + t2
                    tok["qkv_mm"] = mm

                def column(which, r, tc):
                    def run():
                        m, ps, free = take_misc()
                        cols = slice(r * D, (r + 1) * D)
                        mm = product(ps[:, :], [(hi[which][:, c, cols], lo[which][:, c, cols],
                                                 xt_hi[:, c, tc * 512:(tc + 1) * 512],
                                                 xt_lo[:, c, tc * 512:(tc + 1) * 512]) for c in range(CC)],
                                     free + tok["w", n] + tok["xt"], s_misc)
                        dst = [(q[i][:, r, tc * 512:(tc + 1) * 512] if which == 0 else k[i][:, tc * 512:(tc + 1) * 512])
                               for q, k in ((q_hi, k_hi), (q_lo, k_lo))]
                        split(ps, m, mm, dst[0], dst[1], ps[:, :])
                    return run

                def value(q4):
                    def run():
                        m, ps, free = take_misc()
                        for jj in range(4):
                            j = 4 * q4 + jj
                            mm = product(ps[:, jj * D:(jj + 1) * D],
                                         [(xt_hi[:, c, j * P:(j + 1) * P], xt_lo[:, c, j * P:(j + 1) * P],
                                           hi[2][:, c, :], lo[2][:, c, :]) for c in range(CC)],
                                         free + tok["w", n] + tok["xt"], s_misc if jj == 3 else None, first=(jj == 0))
                        split(ps, m, mm, v_hi[i][:, 4 * q4:4 * q4 + 4, 0:D], v_lo[i][:, 4 * q4:4 * q4 + 4, 0:D],
                              ps[:, :].rearrange("p (j d) -> p j d", d=D))
                    return run

                for tc in range(T // 512):
                    tasks += [column(1, 0, tc), column(0, 0, tc), column(0, 1, tc), value(tc)]
                return tasks

            units = []
            for n in range(B * H):
                for g in range(NG):
                    for s in range(2 * g + 2):
                        units.append((n, g, s))
            av_done, made = {}, {}

            def score_tile(u):
                n, g, s = units[u]
                i, ps = n % 2, bank[u % 2]
                t0 = P if s == 2 * g + 1 else 0
                w = GROUP - t0
                dst = ps[:, 0:R * w].rearrange("p (r t) -> p r t", r=R)
                qs = slice(g * GROUP + t0, (g + 1) * GROUP)
                ks = slice(s * P, (s + 1) * P)
                return product(dst, [(k_hi[i][:, ks], k_lo[i][:, ks], q_hi[i][:, :, qs], q_lo[i][:, :, qs])],
                               tok["qkv", n] + made.get(("read", u - 2), []), s_scores)

            def make_a(u, mm):
                n, g, s = units[u]
                b, h = divmod(n, H)
                bi = b % 2
                i3 = u % 3
                w = P if s == 2 * g + 1 else GROUP
                src = bank[u % 2][:, 0:R * w].rearrange("p (r t) -> p r t", r=R)
                raw = a32[u % 2][:, :, 0:w]
                hi, lo = a_hi[i3][:, :, 0:w], a_lo[i3][:, :, 0:w]
                free = av_done.get(u - 3, [])
                raw_free = made.get(("a32", u - 2), [])
                if s < 2 * g:
                    scale = c_s[bi][:, g * (g - 1) + s, h:h + 1]
                    t = act.put(lambda e: e.activation(raw, src, ACT.Square, scale=scale),
                                mm + raw_free + tok["gates", b], s_sq)
                    made["read", u] = t
                else:
                    t = act.put(lambda e: e.activation(raw, src, ACT.Square), mm + raw_free, s_sq)
                    made["read", u] = t
                    decay = (em[n % 2][:, g, 0:GROUP] if s == 2 * g else em[n % 2][:, g, GROUP:GROUP + P])
                    t = dve.put(lambda e: e.tensor_tensor(raw, raw, decay.unsqueeze(1).to_broadcast([P, R, w]),
                                                          ALU.mult), t + tok["em", n], s_a32)
                    tok["head_a32", n] = t
                if u % 2:
                    t = pool.put(lambda e: e.tensor_copy(hi, raw), t + free, s_a_hi_pool)
                else:
                    t = act.put(lambda e: e.activation(hi, raw, ACT.Copy), t + free, s_a_hi)
                t2 = dve.put(lambda e: e.tensor_tensor(lo, raw, f32(hi), ALU.subtract), t + free, s_a_lo)
                made[u] = t + t2
                made["a32", u] = t + t2

            off_free, diag_free = {}, {}

            def value_product(u):
                n, g, s = units[u]
                i, i3 = n % 2, u % 3
                diag = s >= 2 * g
                tts = [1] if s == 2 * g + 1 else [0, 1]
                t_off = P if s == 2 * g + 1 else 0
                for tt in tts:
                    ps = bank[(4 if diag else 2) + tt]
                    free = (diag_free if diag else off_free).get("last", [])
                    dst = ps[:, 0:R * VW].rearrange("p (r v) -> p r v", r=R)
                    first = s == (2 * g if diag else 0)
                    for r in range(R):
                        cols = slice(tt * P - t_off, (tt + 1) * P - t_off)
                        av_done[u] = product(dst[:, r, :], [(a_hi[i3][:, r, cols], a_lo[i3][:, r, cols],
                                                            v_hi[i][:, s, :], v_lo[i][:, s, :])],
                                             made[u] + free, s_av if (tt, r) == (tts[-1], R - 1) else None,
                                             first=first and r == 0)
                tok["av", n] = av_done[u]
                if s == 2 * g - 1:
                    for tt in range(2):
                        t = act.put(lambda e, tt=tt: e.activation(offs[:, tt, :, :], bank[2 + tt][:, 0:R * VW].rearrange(
                            "p (r v) -> p r v", r=R), ACT.Copy), av_done[u] + tok.get("num", []), s_off)
                    off_free["last"] = t
                    tok["off"] = t

            def normalise(n, g, done):
                b, h = divmod(n, H)
                bi = b % 2
                for tt in range(2):
                    dg = bank[4 + tt][:, 0:R * VW].rearrange("p (r v) -> p r v", r=R)
                    if g == 0:
                        t = dve.put(lambda e, tt=tt, dg=dg: e.tensor_copy(num[:, tt, :, :], dg), done, s_num)
                    else:
                        t = dve.put(lambda e, tt=tt, dg=dg: e.scalar_tensor_tensor(
                            out=num[:, tt, :, :], in0=offs[:, tt, :, :], scalar=f_t[bi][:, 2 * g + tt, h:h + 1],
                            in1=dg, op0=ALU.mult, op1=ALU.add), done + tok["off"] + tok["gates", b], s_num)
                diag_free["last"] = t
                tok["num"] = t
                t = dve.put(lambda e: e.tensor_scalar(nrm[:, :, :], num[:, :, :, D], NORM_EPS, None, ALU.add), t, s_y)
                t = dve.put(lambda e: e.reciprocal(rec[:, :, :], nrm[:, :, :]), t, s_y)
                return dve.put(lambda e: e.tensor_tensor(
                    y_n[:, :, :, :].rearrange("p k r d -> p (k r) d"),
                    num[:, :, :, 0:D].rearrange("p k r d -> p (k r) d"),
                    rec[:, :, :].rearrange("p k r -> p (k r)").unsqueeze(2).to_broadcast([P, 2 * R, D]), ALU.mult),
                    t + tok.get("y_read", []), s_y)

            def turn(n, g, ready):
                m, ps, free = take_misc()
                for tt in range(2):
                    for r in range(R):
                        mm = pe.put(lambda e, tt=tt, r=r, ps=ps: e.transpose(
                            ps[:, r * GROUP + tt * P:r * GROUP + (tt + 1) * P], y_n[:, tt, r, :], ident),
                            ready + free + const_in, s_misc if (tt, r) == (1, R - 1) else None)
                tok["y_read"] = mm
                src = ps[:, :].rearrange("p (r t) -> p r t", r=R)
                t = act.put(lambda e: e.activation(yt_hi[:, :, :], src, ACT.Copy), mm + tok.get("yt_read", []), s_yt_hi)
                t2 = dve.put(lambda e: e.tensor_tensor(yt_lo[:, :, :], src, f32(yt_hi[:, :, :]), ALU.subtract),
                             mm + t, s_yt_lo)
                misc["free"][m] = t + t2
                return t + t2

            def project(n, g, ready):
                b = n // H
                hi, lo = wc_hi[n % 2], wc_lo[n % 2]
                m, ps, free = take_misc()
                for tt in range(2):
                    ts = slice(tt * P, (tt + 1) * P)
                    mm = product(ps[:, tt * C:(tt + 1) * C], [(yt_hi[:, r, ts], yt_lo[:, r, ts], hi[:, r, :], lo[:, r, :])
                                                              for r in range(R)],
                                 ready + free, s_misc if tt else None, first=(tt == 0))
                tok["yt_read"] = tok["proj", n] = mm
                part = acc[b % 2][:, 2 * g:2 * g + 2, :]
                t = dve.put(lambda e: e.tensor_tensor(part, ps[:, :].rearrange("p (j c) -> p j c", c=C), part, ALU.add),
                            mm + tok["acc0", b] + tok.get(("acc", b, g), []), s_acc)
                misc["free"][m] = t
                tok["acc", b, g] = t
                tok["acc", b] = t

            def route_tasks(b):
                i = b % 2
                st = {}
                L, Q = s_ln, s_route

                def layer_norm():
                    for j in range(TILES):
                        dve.put(lambda e, j=j: e.bn_stats(stats[:, j, :], acc[i][:, j, :]), tok["acc", b], L)
                    t = [(L, L.count)]
                    for j in range(TILES):
                        t = dve.put(lambda e, j=j: e.bn_aggr(mv[:, j, :], stats[:, j, :]), t, L)
                    t = dve.put(lambda e: e.tensor_scalar(std[:, :], mv[:, :, 1], LN_EPS, None, ALU.add), t, L)
                    t = act.put(lambda e: e.activation(std[:, :], std[:, :], ACT.Sqrt), t, s_ln_act)
                    t = dve.put(lambda e: e.reciprocal(rstd[:, :], std[:, :]), t, L)
                    for j in range(TILES):
                        t = dve.put(lambda e, j=j: e.tensor_scalar(rows[:, j, 0:C], acc[i][:, j, :], mv[:, j, 0:1],
                                                                   rstd[:, j:j + 1], ALU.subtract, ALU.mult),
                                    t + tok.get("rows_read", []), L)
                    st["x1"] = tok["ln", b] = t
                    sp.put(lambda e: e.dma_start(x1_dram[b * T:(b + 1) * T, :].rearrange("(j p) c -> p j c", p=P),
                                                 rows[:, :, 0:C]), t, s_x1_out)
                    st["token"] = pool.put(lambda e: e.iota(rows[:, :, TOKEN_COL].bitcast(I32), pattern=[[P, TILES]],
                                                            base=b * T, channel_multiplier=1),
                                           tok.get("rows_read", []), s_rows_pool)

                def turn_x1(k):
                    def run():
                        m, ps, free = take_misc()
                        for jj in range(2):
                            for c in range(CC):
                                mm = pe.put(lambda e, jj=jj, c=c: e.transpose(
                                    ps[:, c * GROUP + jj * P:c * GROUP + (jj + 1) * P],
                                    rows[:, 2 * k + jj, c * P:(c + 1) * P], ident),
                                    st["x1"] + free, s_misc if (jj, c) == (1, CC - 1) else None)
                        src = ps[:, :].rearrange("p (c t) -> p c t", c=CC)
                        hi, lo = x1t_hi, x1t_lo
                        t = act.put(lambda e: e.activation(hi[:, :, :], src, ACT.Copy),
                                    mm + tok.get("x1t_read", []), s_x1t_hi)
                        t2 = dve.put(lambda e: e.tensor_tensor(lo[:, :, :], src, f32(hi[:, :, :]),
                                                               ALU.subtract), mm + t, s_x1t_lo)
                        misc["free"][m] = t + t2
                        ts = slice(b * T + k * GROUP, b * T + (k + 1) * GROUP)
                        sp.put(lambda e: e.dma_start(x1t_dram[0, :, :, ts], f32(hi[:, :, :])), t, s_x1t_out)
                        stored = sp.put(lambda e: e.dma_start(x1t_dram[1, :, :, ts], f32(lo[:, :, :])), t2,
                                        s_x1t_out)
                        m, ps_lg, free = take_misc()
                        lg = ps_lg[:, 0:2 * E].rearrange("p (j e) -> p j e", e=E)
                        for jj in range(2):
                            js = slice(jj * P, (jj + 1) * P)
                            mm = product(lg[:, jj, :], [(hi[:, c, js], lo[:, c, js], gw_hi[:, c, :], gw_lo[:, c, :])
                                                        for c in range(CC)],
                                         t + t2 + free + tab_ready, s_misc if jj else None, first=(jj == 0))
                        tok["x1t_read"] = stored + mm
                        t = dve.put(lambda e: e.tensor_copy(shifted[:, 2 * k:2 * k + 2, :], lg), mm, s_route)
                        misc["free"][m] = t
                        st["logit"] = t
                    return run

                def logits():
                    lg = shifted[:, :, :]
                    mm = st["logit"]
                    wide = lambda v: v[:, :].unsqueeze(2).to_broadcast([P, TILES, E])
                    t = dve.put(lambda e: e.tensor_reduce(row_max[:, :], lg, AX.X, ALU.max), mm, Q)
                    t = dve.put(lambda e: e.tensor_tensor(shifted[:, :, :], lg, wide(row_max), ALU.subtract), t, Q)
                    t = act.put(lambda e: e.activation(shifted[:, :, :], shifted[:, :, :], ACT.Exp), t, s_route_act)
                    t = dve.put(lambda e: e.tensor_reduce(row_sum[:, :], shifted[:, :, :], AX.X, ALU.add), t, Q)
                    t = dve.put(lambda e: e.reciprocal(row_rec[:, :], row_sum[:, :]), t, Q)
                    st["t"] = dve.put(lambda e: e.tensor_tensor(scores[:, :, :], shifted[:, :, :], wide(row_rec),
                                                                ALU.mult), t, Q)

                def top():
                    t = st["t"]
                    for j in range(TILES):
                        dve.put(lambda e, j=j: e.max(out=top8[:, j, :], in_=scores[:, j, :]), t, Q)
                    t = [(Q, Q.count)]
                    for j in range(TILES):
                        dve.put(lambda e, j=j: e.max_index(out=top8_at[:, j, :], in_max=top8[:, j, :],
                                                           in_values=scores[:, j, :]), t, Q)
                    t = [(Q, Q.count)]
                    t = dve.put(lambda e: e.tensor_copy(chosen_at[:, :, :], top8_at[:, :, 0:TOPK]), t, Q)
                    q4 = TILES // 4
                    iota = tab[:, K_IOTA:K_IOTA + E].unsqueeze(1).to_broadcast([P, q4 * TOPK, E])
                    for q in range(4):
                        js = slice(q * q4, (q + 1) * q4)
                        t = dve.put(lambda e, js=js: e.tensor_tensor(
                            onehot[:, :, :], chosen_at[:, js, :].rearrange("p j k -> p (j k)").unsqueeze(2)
                            .to_broadcast([P, q4 * TOPK, E]), iota, ALU.is_equal), t, Q)
                        t = dve.put(lambda e, js=js: e.tensor_reduce(
                            chosen[:, js, :], onehot[:, :, :].rearrange("p (j k) e -> p j e k", k=TOPK), AX.X,
                            ALU.add), t, Q)
                    st["t"] = dve.put(lambda e: e.tensor_copy(chosen_bf[:, :, :], chosen[:, :, :]), t, Q)

                def count():
                    m, ps, free = take_misc()
                    before = ps[:, :].rearrange("p (j e) -> p j e", e=E)
                    pe.put(lambda e: e.matmul(before, strict_bf[:, :], chosen_bf[:, :, :], start=True, stop=False,
                                              skip_group_check=True), st["t"] + free + tab_ready + ones_ready)
                    for j in range(TILES - 1):
                        mm = pe.put(lambda e, j=j: e.matmul(
                            before[:, j + 1:TILES, :], ones_bf[:, :],
                            chosen_bf[:, j:j + 1, :].to_broadcast([P, TILES - 1 - j, E]), start=False,
                            stop=(j == TILES - 2), skip_group_check=True), (), s_misc if j == TILES - 2 else None)
                    t = dve.put(lambda e: e.tensor_tensor(
                        slot_of[:, :, :], before, taken[:, :].unsqueeze(1).to_broadcast([P, TILES, E]), ALU.add),
                        mm + ones_ready, Q)
                    misc["free"][m] = t
                    m, ps2, free = take_misc()
                    for j in range(TILES):
                        mm = pe.put(lambda e, j=j: e.matmul(ps2[:, 0:E], ones_bf[:, :], chosen_bf[:, j, :],
                                                            start=(j == 0), stop=(j == TILES - 1)),
                                    free, s_misc if j == TILES - 1 else None)
                    dve.put(lambda e: e.tensor_tensor(taken[:, :], ps2[:, 0:E], taken[:, :], ALU.add), mm + t, Q)
                    misc["free"][m] = [(Q, Q.count)]
                    t = dve.put(lambda e: e.tensor_scalar(over[:, :, :], slot_of[:, :, :], float(CAP), float(NOWHERE),
                                                          ALU.is_ge, ALU.mult), t, Q)
                    t = dve.put(lambda e: e.tensor_tensor(
                        slot_of[:, :, :], slot_of[:, :, :],
                        tab[:, K_BASE:K_BASE + E].unsqueeze(1).to_broadcast([P, TILES, E]), ALU.add), t, Q)
                    st["t"] = dve.put(lambda e: e.tensor_tensor(slot_of[:, :, :], slot_of[:, :, :], over[:, :, :],
                                                                ALU.add), t, Q)

                def slot_numbers():
                    t = st["t"]
                    q4 = TILES // 4
                    iota = tab[:, K_IOTA:K_IOTA + E].unsqueeze(1).to_broadcast([P, q4 * TOPK, E])
                    for q in range(4):
                        js = slice(q * q4, (q + 1) * q4)
                        t = dve.put(lambda e, js=js: e.tensor_tensor(
                            onehot[:, :, :], chosen_at[:, js, :].rearrange("p j k -> p (j k)").unsqueeze(2)
                            .to_broadcast([P, q4 * TOPK, E]), iota, ALU.is_equal), t, Q)
                        for jj in range(q4):
                            t2 = dve.put(lambda e, j=q * q4 + jj, jj=jj: e.tensor_tensor(
                                onehot[:, jj * TOPK:(jj + 1) * TOPK, :], onehot[:, jj * TOPK:(jj + 1) * TOPK, :],
                                slot_of[:, j:j + 1, :].to_broadcast([P, TOPK, E]), ALU.mult), t, Q)
                        t = dve.put(lambda e, js=js: e.tensor_reduce(
                            slot_f[:, js, :].rearrange("p j k -> p (j k)"), onehot[:, :, :], AX.X, ALU.add), t2, Q)
                    st["slot"] = dve.put(lambda e: e.tensor_copy(slot_u[:, :, :], slot_f[:, :, :]),
                                         t + tok.get("rows_read", []), Q)
                    t = dve.put(lambda e: e.tensor_tensor(scores[:, :, :], scores[:, :, :], chosen[:, :, :], ALU.mult),
                                (), Q)
                    t = dve.put(lambda e: e.tensor_reduce(top_sum[:, :], scores[:, :, :], AX.X, ALU.add), t, Q)
                    t = dve.put(lambda e: e.tensor_scalar(top_sum[:, :], top_sum[:, :], TOPK_EPS, None, ALU.add), t, Q)
                    t = dve.put(lambda e: e.reciprocal(top_rec[:, :], top_sum[:, :]), t, Q)
                    st["w"] = dve.put(lambda e: e.tensor_tensor(
                        rows[:, :, C:C + E], scores[:, :, :], top_rec[:, :].unsqueeze(2).to_broadcast([P, TILES, E]),
                        ALU.mult), t + tok.get("rows_read", []), Q)

                def scatter(j):
                    def run():
                        for k in range(TOPK):
                            t = pool.put(lambda e, k=k: e.indirect_dma_start(
                                out=slots, out_offset=bass.IndirectOffsetOnAxis(ap=slot_u[:, j, k:k + 1], axis=0),
                                in_=rows[:, j, :], in_offset=None, bounds_check=E * CAP - 1, oob_is_err=False),
                                st["slot"] + st["w"] + st["token"] + [(s_slots0, 16 * E)] + ones_ready, s_scatter)
                        tok["scatter"] = t
                        tok["rows_read"] = t + [(s_x1_out, s_x1_out.count)]
                    return run

                return ([layer_norm] + [turn_x1(k) for k in range(NG)] + [logits, top, count, slot_numbers]
                        + [scatter(j) for j in range(TILES)])

            prepare_batch(0)
            load_weights(0)
            gates(0)
            decay_matrices(0)
            for task in qkv_tasks(0):
                task()
            late = []
            upto = {n: max(u for u, x_ in enumerate(units) if x_[0] == n) for n in range(B * H)}
            mm_of = {0: score_tile(0)}
            make_a(0, mm_of[0])
            mm_of[1] = score_tile(1)
            make_a(1, mm_of[1])
            background = []
            must = []
            for u, (n, g, s) in enumerate(units):
                if (g, s) == (0, 0):
                    assert not must
                    if n + 1 < B * H:
                        if (n + 1) % H == 0:
                            pass
                        if (n + 1) // H != n // H:
                            must.append(lambda b=(n + 1) // H: prepare_batch(b))
                            must.append(lambda b=(n + 1) // H: gates(b))
                        must.append(lambda n=n: decay_matrices(n + 1))
                        load_weights(n + 1)
                        must += qkv_tasks(n + 1)
                    if n < E // 8 * 1:
                        for ex in range(n * E // H, (n + 1) * E // H):
                            sp.put(lambda e, ex=ex: e.dma_start(
                                slots[ex * CAP:(ex + 1) * CAP, :].rearrange("(j p) c -> p j c", p=P), slot0[:, :, :]),
                                slot0_ready, s_slots0)
                left = 18 - sum(2 * k + 2 for k in range(g)) - s
                if must and (len(must) >= left or u % 2 == 0):
                    must.pop(0)()
                    if len(must) > left:
                        must.pop(0)()
                elif background and not (must and n % H == H - 1):
                    background.pop(0)()
                if u + 2 < len(units):
                    if units[u + 2][0] != n:
                        while must:
                            must.pop(0)()
                    mm_of[u + 2] = score_tile(u + 2)
                    make_a(u + 2, mm_of[u + 2])
                value_product(u)
                if s == 2 * g + 1:
                    ready = normalise(n, g, av_done[u])
                    late.append((u + 1, "turn", n, g, ready))
                for item in [x_ for x_ in late if x_[0] <= u or u == len(units) - 1]:
                    late.remove(item)
                    if item[1] == "turn":
                        ready = turn(item[2], item[3], item[4])
                        late.append((u + 2, "project", item[2], item[3], ready))
                    else:
                        project(item[2], item[3], item[4])
                if u == upto[n]:
                    tok["heads", n // H] = av_done[u] + tok["num"]
                    if True:
                        late_proj = [x_ for x_ in late if x_[2] == n]
                        for item in sorted(late_proj, key=lambda x_: x_[0]):
                            late.remove(item)
                            if item[1] == "turn":
                                project(item[2], item[3], turn(item[2], item[3], item[4]))
                            else:
                                project(item[2], item[3], item[4])
                    if n % H == H - 1 and n + 1 < B * H:
                        while background:
                            background.pop(0)()
                        background = route_tasks(n // H)
            while late:
                item = late.pop(0)
                if item[1] == "turn":
                    late.append((0, "project", item[2], item[3], turn(item[2], item[3], item[4])))
                else:
                    project(item[2], item[3], item[4])
            for task in background + route_tasks(B - 1):
                task()
            att_done = (tok["proj", B * H - 1] + [(s, s.count) for s in (
                s_acc, s_yt_hi, s_a_hi, s_a_hi_pool, s_a_lo, s_y, s_w_split, s_mask_act, s_num, s_off, s_av, s_acc0,
                s_gate_act, s_gate_dve, s_qkv_lo, s_slots0, s_decay_out)])

        with ExitStack() as ffn:
            WS = 3
            gu_raw = [sb(ffn, f"gu_raw{i}", [P, CC, 2 * F]) for i in range(2)]
            da_raw = [sb(ffn, f"da_raw{i}", [P, C]) for i in range(2)]
            db_raw = [sb(ffn, f"db_raw{i}", [P, C]) for i in range(2)]
            gu_hi = [sb(ffn, f"gu_hi{i}", [P, CC, GU], F32R) for i in range(WS)]
            gu_lo = [sb(ffn, f"gu_lo{i}", [P, CC, GU], F32R) for i in range(WS)]
            dn_hi = [sb(ffn, f"dn_hi{i}", [P, 2, C], F32R) for i in range(WS)]
            dn_lo = [sb(ffn, f"dn_lo{i}", [P, 2, C], F32R) for i in range(WS)]
            xr = [sb(ffn, f"xr{i}", [P, CT, ROW]) for i in range(2)]
            xe_hi = [sb(ffn, f"xe_hi{i}", [P, CC, CAP], F32R) for i in range(2)]
            xe_lo = [sb(ffn, f"xe_lo{i}", [P, CC, CAP], F32R) for i in range(2)]
            silu_a = sb(ffn, "silu_a", [P, TOKC])
            silu_b = sb(ffn, "silu_b", [FB, TOKC])
            h_a = sb(ffn, "h_a", [P, TOKC])
            h_b = sb(ffn, "h_b", [FB, TOKC])
            ha_hi = [sb(ffn, f"ha_hi{i}", [P, TOKC], F32R) for i in range(2)]
            ha_lo = [sb(ffn, f"ha_lo{i}", [P, TOKC], F32R) for i in range(2)]
            hb = [sb(ffn, f"hb{i}", [FBO + FB, TOKC], F32R) for i in range(2)]
            y_e = [sb(ffn, f"y_e{i}", [P, CT, C]) for i in range(2)]
            x1_r = xr

            c_raw = [signal(f"c_raw{i}", 16) for i in range(2)]
            c_zero, c_split, c_split_d = signal("c_zero"), signal("c_split"), signal("c_split_d")
            c_x = [signal(f"c_x{i}", 16) for i in range(2)]
            c_r = [signal(f"c_r{i}", 16) for i in range(2)]
            c_xh, c_xl, c_t = signal("c_xh"), signal("c_xl"), signal("c_t")
            c_gu, c_silu, c_h, c_hh, c_hl, c_dn, c_y = (signal(k) for k in (
                "c_gu", "c_silu", "c_h", "c_hh", "c_hl", "c_dn", "c_y"))
            c_store = signal("c_store", 16)
            c_yd = signal("c_yd")
            c_add = signal("c_add", 16)

            for i in range(2):
                pool.put(lambda e, i=i: e.memset(db_raw[i][:, :], 0.0), att_done, c_zero)
                pool.put(lambda e, i=i: e.memset(f32(hb[i][:, :]), 0.0), (), c_zero)
            for i in range(WS):
                pool.put(lambda e, i=i: e.memset(f32(gu_hi[i][:, :, :]), 0.0), (), c_zero)
                pool.put(lambda e, i=i: e.memset(f32(gu_lo[i][:, :, :]), 0.0), (), c_zero)
            zero = pool.put(lambda e: e.memset(y_e[0][:, :, :], 0.0), (), c_zero)
            spare = sp.put(lambda e: e.dma_start(y_dram[N:N + CAP, :].rearrange("(j p) c -> p j c", p=P),
                                                 y_e[0][:, :, :]), zero, c_store)
            for q in (sp, act, dve, pe):
                q.reached.update()
            use = {}

            def ffn_weights(w, x_id):
                i = use["raw_n"] = (use.get("raw_n", -1) + 1) % 2
                need = att_done + zero + use.get(("raw", i), [])
                sp.put(lambda e: e.dma_start(gu_raw[i][:, :, :], wgu[x_id]), need, c_raw[i])
                sp.put(lambda e: e.dma_start(da_raw[i][:, :], wdn[x_id, 0:P, :]), (), c_raw[i])
                sp.put(lambda e: e.dma_start(db_raw[i][0:FB, :], wdn[x_id, P:F, :]), (), c_raw[i])
                got = sp.put(lambda e: e.dma_start(db_raw[i][FBO:FBO + FB, :], wdn[x_id, P:F, :]), (), c_raw[i])
                free = use.get(("w_read", w), [])
                K = FBO + FB
                tail = lambda a: a[:, :, 2 * P:2 * F].rearrange("p c (k f) -> p c k f", k=2)

                def gapped(a, k):
                    o = 2 * P + k * FBO
                    return a[:, :, o:o + FB]
                for (hi, src) in ((gu_hi[w][:, :, 0:2 * P], gu_raw[i][:, :, 0:2 * P]),
                                  (gapped(gu_hi[w], 0), gu_raw[i][:, :, 2 * P:2 * P + FB]),
                                  (gapped(gu_hi[w], 1), gu_raw[i][:, :, 2 * P + FB:2 * F]),
                                  (dn_hi[w][:, 0, :], da_raw[i][:, :]),
                                  (dn_hi[w][0:K, 1, :], db_raw[i][0:K, :])):
                    t = pool.put(lambda e, hi=hi, src=src: e.tensor_copy(hi, src), got + free, c_split)
                for (lo, hi, src) in ((gu_lo[w][:, :, 0:2 * P], gu_hi[w][:, :, 0:2 * P], gu_raw[i][:, :, 0:2 * P]),
                                      (gapped(gu_lo[w], 0), gapped(gu_hi[w], 0), gu_raw[i][:, :, 2 * P:2 * P + FB]),
                                      (gapped(gu_lo[w], 1), gapped(gu_hi[w], 1), gu_raw[i][:, :, 2 * P + FB:2 * F]),
                                      (dn_lo[w][:, 0, :], dn_hi[w][:, 0, :], da_raw[i][:, :]),
                                      (dn_lo[w][0:K, 1, :], dn_hi[w][0:K, 1, :], db_raw[i][0:K, :])):
                    t2 = dve.put(lambda e, lo=lo, hi=hi, src=src: e.tensor_tensor(lo, src, f32(hi), ALU.subtract),
                                 t + got + free, c_split_d)
                use["raw", i] = t + t2
                use["w", w] = t + t2

            gu_free = [[], []]

            def gate_up(k, w, x_hi, x_lo, width, ready):
                b0 = 3 * (k % 2)
                parts = [(bank[b0], slice(0, P)), (bank[b0 + 1], slice(P, 2 * P)), (bank[b0 + 2], slice(2 * P, GU))]
                mms = []
                for ps, cols in parts:
                    m = cols.stop - cols.start
                    mms.append(product(ps[0:m, 0:width], [(gu_hi[w][:, c, cols], gu_lo[w][:, c, cols], x_hi[:, c, :],
                                                           x_lo[:, c, :]) for c in range(CC)],
                                       ready + use["w", w] + gu_free[k % 2] + att_done, c_gu))
                i = k % 2
                free = use.get(("h", i), [])
                ga, ua = bank[b0][:, 0:width], bank[b0 + 1][:, 0:width]
                gb, ub = bank[b0 + 2][0:FB, 0:width], bank[b0 + 2][FBO:FBO + FB, 0:width]
                sa, sb_ = silu_a[:, 0:width], silu_b[:, 0:width]
                ha, hb32 = h_a[:, 0:width], h_b[:, 0:width]
                t1 = act.put(lambda e: e.activation(sa, ga, ACT.Silu), mms[0] + use.get("h32a", []) + att_done, c_silu)
                t2 = act.put(lambda e: e.activation(sb_, gb, ACT.Silu), mms[2] + use.get("h32b", []), c_silu)
                d1 = dve.put(lambda e: e.tensor_tensor(ha, ua, sa, ALU.mult), mms[1] + t1 + use.get("h_read", []) + att_done,
                             c_h)
                d2 = dve.put(lambda e: e.tensor_tensor(hb32, ub, sb_, ALU.mult), mms[2] + t2, c_h)
                use["h32a"], use["h32b"] = d1, d2
                gu_free[i] = d2 + t2
                a1 = act.put(lambda e: e.activation(ha_hi[i][:, 0:width], ha, ACT.Copy), d1 + free, c_hh)
                a2 = act.put(lambda e: e.activation(hb[i][0:FB, 0:width], hb32, ACT.Copy), d2 + free + zero, c_hh)
                l1 = dve.put(lambda e: e.tensor_tensor(ha_lo[i][:, 0:width], ha, f32(ha_hi[i][:, 0:width]), ALU.subtract),
                             a1 + d1 + free, c_hl)
                l2 = dve.put(lambda e: e.tensor_tensor(hb[i][FBO:FBO + FB, 0:width], hb32, f32(hb[i][0:FB, 0:width]),
                                                       ALU.subtract), a2 + d2 + zero, c_hl)
                use["h_read"] = l2
                return a2 + l2

            def down(ks, ws, t0, dst, needs, tells, first):
                mms = []
                for k, w in zip(ks, ws):
                    i, ts, K = k % 2, slice(t0, t0 + P), FBO + FB
                    mms += [(ha_hi[i][:, ts], dn_hi[w][:, 0, :]), (ha_hi[i][:, ts], dn_lo[w][:, 0, :]),
                            (ha_lo[i][:, ts], dn_hi[w][:, 0, :]),
                            (hb[i][:, ts], dn_hi[w][0:K, 1, :]), (hb[i][:, ts], dn_lo[w][0:K, 1, :])]
                for n, (a, b_) in enumerate(mms):
                    done = pe.put(lambda e, a=a, b_=b_, n=n: e.matmul(dst, a, b_, start=(first and n == 0),
                                                                      stop=(n == len(mms) - 1), skip_group_check=True),
                                  needs if n == 0 else (), tells if n == len(mms) - 1 else None)
                return done

            for w in range(2):
                ffn_weights(w, E + w)
            x1_stored = [(q, q.count) for q in (s_x1_out, s_x1t_out)]
            stored = spare
            k = 0
            ready_of, job = {}, {}

            def shared_load(m):
                i = m % 2
                ms = slice(m * TOKC, (m + 1) * TOKC)
                need = x1_stored + use.get(("xe", i), []) + att_done
                sp.put(lambda e: e.dma_start(f32(xe_hi[i][:, :, 0:TOKC]), x1t_dram[0, :, :, ms]), need, c_x[i])
                job["x", m] = sp.put(lambda e: e.dma_start(f32(xe_lo[i][:, :, 0:TOKC]), x1t_dram[1, :, :, ms]), (), c_x[i])
                job["r", m] = sp.put(lambda e: e.dma_start(
                    xr[i][:, 0:TOKC // P, 0:C], x1_dram[ms, :].rearrange("(j p) c -> p j c", p=P)),
                    use.get(("xr", i), []), c_r[i])

            def shared_up(m):
                nonlocal k
                i = m % 2
                job["k", m] = [k, k + 1]
                r = []
                for w in range(2):
                    ready_of[k] = gate_up(k, w, xe_hi[i][:, :, 0:TOKC], xe_lo[i][:, :, 0:TOKC], TOKC, job["x", m])
                    k += 1
                use["xe", i] = [(c_gu, c_gu.count)]

            def shared_down(m):
                nonlocal stored
                i = m % 2
                ks = job["k", m]
                for pair in range(TOKC // GROUP):
                    q, ps, free = take_misc()
                    for jj in range(2):
                        t0 = (2 * pair + jj) * P
                        mm = down(ks, [0, 1], t0, ps[:, jj * C:(jj + 1) * C], ready_of[ks[0]] + ready_of[ks[1]] + free,
                                  c_dn, jj == 0)
                    t = dve.put(lambda e, ps=ps, pair=pair: e.tensor_tensor(
                        y_e[i][:, 2 * pair:2 * pair + 2, :], ps[:, :].rearrange("p (j c) -> p j c", c=C),
                        xr[i][:, 2 * pair:2 * pair + 2, 0:C], ALU.add), mm + job["r", m] + use.get(("y", i), []) + spare,
                        c_yd)
                    misc["free"][q] = t
                for kk in ks:
                    use["h", kk % 2] = mm
                use["xr", i] = t
                use["w_read", 0] = use["w_read", 1] = mm
                stored = sp.put(lambda e: e.dma_start(y_dram[m * TOKC:(m + 1) * TOKC, :].rearrange(
                    "(j p) c -> p j c", p=P), y_e[i][:, 0:TOKC // P, :]), t, c_store)
                use["y", i] = stored

            scattered = tok["scatter"]
            HALF = CAP // 2

            def expert_load(x_id):
                i = x_id % 2
                job["xr", x_id] = sp.put(lambda e: e.dma_start(xr[i][:, :, :], slots[x_id * CAP:(x_id + 1) * CAP, :]
                                                               .rearrange("(j p) c -> p j c", p=P)),
                                         scattered + use.get(("xr", i), []), c_r[i])

            def expert_turn(x_id):
                i = x_id % 2
                for pair in range(CT // 2):
                    q, ps, free = take_misc()
                    for jj in range(2):
                        for c in range(CC):
                            mm = pe.put(lambda e, jj=jj, c=c, ps=ps, pair=pair: e.transpose(
                                ps[:, c * GROUP + jj * P:c * GROUP + (jj + 1) * P],
                                xr[i][:, 2 * pair + jj, c * P:(c + 1) * P], ident),
                                job["xr", x_id] + free, c_t if (jj, c) == (1, CC - 1) else None)
                    src = ps[:, :].rearrange("p (c t) -> p c t", c=CC)
                    ts = slice(pair * GROUP, (pair + 1) * GROUP)
                    free = use.get(("xe", i), [])
                    t = act.put(lambda e, src=src, ts=ts: e.activation(xe_hi[i][:, :, ts], src, ACT.Copy), mm + free, c_xh)
                    t2 = dve.put(lambda e, src=src, ts=ts: e.tensor_tensor(xe_lo[i][:, :, ts], src, f32(xe_hi[i][:, :, ts]),
                                                                           ALU.subtract), mm + t + free, c_xl)
                    misc["free"][q] = t + t2
                job["xe", x_id] = t + t2

            def expert_up(x_id, half):
                nonlocal k
                i = x_id % 2
                ts = slice(half * HALF, (half + 1) * HALF)
                ready_of[k] = gate_up(k, (x_id + 2) % WS, xe_hi[i][:, :, ts], xe_lo[i][:, :, ts], HALF, job["xe", x_id])
                job["k", x_id, half] = k
                k += 1
                use["xe", i] = [(c_gu, c_gu.count)]

            def expert_down(x_id, half):
                i, kk = x_id % 2, job["k", x_id, half]
                w = (x_id + 2) % WS
                for jj in range(HALF // P):
                    j = half * (HALF // P) + jj
                    q, ps, free = take_misc()
                    mm = down([kk], [w], jj * P, ps[:, 0:C], ready_of[kk] + free, c_dn, True)
                    t = act.put(lambda e, j=j, ps=ps: e.activation(y_e[i][:, j, :], ps[:, 0:C], ACT.Copy,
                                                                   scale=xr[i][:, j, C + x_id:C + x_id + 1]),
                                mm + use.get(("y", i), []), c_y)
                    misc["free"][q] = t
                    added = pool.put(lambda e, j=j: e.indirect_dma_start(
                        out=y_dram, out_offset=bass.IndirectOffsetOnAxis(ap=xr[i][:, j, TOKEN_COL:TOKEN_COL + 1].bitcast(U32),
                                                                         axis=0),
                        in_=y_e[i][:, j, :], in_offset=None, bounds_check=N + CAP - 1, oob_is_err=True,
                        compute_op=ALU.add), t + stored + use.get("added", []), c_add)
                use["h", kk % 2] = mm
                use["w_read", w] = mm
                if half:
                    use["added"] = added
                    use["y", i] = use["xr", i] = added

            shared_load(0)
            shared_load(1)
            M = N // TOKC
            for m in range(M):
                shared_up(m)
                shared_down(m)
                if m + 2 < M:
                    shared_load(m + 2)
                if m == M - 2:
                    ffn_weights(2, 0)
            expert_load(0)
            expert_load(1)
            expert_turn(0)
            ffn_weights(0, 1)
            for x_id in range(E):
                expert_up(x_id, 0)
                if x_id:
                    expert_down(x_id - 1, 1)
                    if x_id + 1 < E:
                        expert_load(x_id + 1)
                        ffn_weights((x_id + 3) % WS, x_id + 1)
                expert_up(x_id, 1)
                if x_id + 1 < E:
                    expert_turn(x_id + 1)
                expert_down(x_id, 0)
            expert_down(E - 1, 1)

            d_in = [signal(f"d_in{i}", 16) for i in range(2)]
            d_dve, d_act = signal("d_dve"), signal("d_act")
            d_out = signal("d_out", 16)
            for b in range(B):
                i = b % 2
                got = sp.put(lambda e, b=b, i=i: e.dma_start(acc[i][:, :, :], y_dram[b * T:(b + 1) * T, :].rearrange(
                    "(j p) c -> p j c", p=P)), use["added"] + tok["ln", B - 1] + tok["ln", B - 2]
                    + tok.get(("out", b - 2), []), d_in[i])
                for j in range(TILES):
                    dve.put(lambda e, j=j, i=i: e.bn_stats(stats[:, j, :], acc[i][:, j, :]), got, d_dve)
                t = [(d_dve, d_dve.count)]
                for j in range(TILES):
                    t = dve.put(lambda e, j=j: e.bn_aggr(mv[:, j, :], stats[:, j, :]), t, d_dve)
                t = dve.put(lambda e: e.tensor_scalar(std[:, :], mv[:, :, 1], LN_EPS, None, ALU.add), t, d_dve)
                t = act.put(lambda e: e.activation(std[:, :], std[:, :], ACT.Sqrt), t, d_act)
                t = dve.put(lambda e: e.reciprocal(rstd[:, :], std[:, :]), t, d_dve)
                for j in range(TILES):
                    t = dve.put(lambda e, j=j, i=i: e.tensor_scalar(acc[i][:, j, :], acc[i][:, j, :], mv[:, j, 0:1],
                                                                    rstd[:, j:j + 1], ALU.subtract, ALU.mult), t, d_dve)
                tok["out", b] = sp.put(lambda e, b=b, i=i: e.dma_start(out[b * T:(b + 1) * T, :].rearrange(
                    "(j p) c -> p j c", p=P), acc[i][:, :, :]), t, d_out)
            for s in (d_out, c_store, s_x1_out, s_x1t_out, s_decay_out, s_slots0):
                sp.items.append(([(s.sem, s.count)], lambda e: None, None))
            for s in (s_scatter, c_add):
                pool.items.append(([(s.sem, s.count)], lambda e: None, None))

        block = ctx.enter_context(nc.Block())
        block.sync(lambda e: sp.emit(e))
        block.gpsimd(lambda e: pool.emit(e))
        block.scalar(lambda e: act.emit(e))
        block.vector(lambda e: dve.emit(e))
        block.tensor(lambda e: pe.emit(e))


def constants(np):
    t = np.zeros((P, K_END), np.float32)
    k, c = np.arange(P)[:, None], np.arange(P)[None, :]
    t[:, K_ID:K_ID + P] = k == c
    t[:, K_TRI:K_TRI + P] = k <= c
    t[:, K_STRICT:K_STRICT + P] = k < c
    t[:, K_MASK:K_MASK + P] = np.where(k <= c, 0.0, NEG)
    t[:, K_BASE:K_BASE + E] = np.arange(E) * CAP
    t[:, K_IOTA:K_IOTA + E] = np.arange(E)
    return t


def kernel(**inputs):
    import numpy as np
    import concourse.bacc as bacc
    from concourse.bass_utils import run_bass_kernel_spmd as run

    get = lambda name: np.asarray(inputs[name])
    x = np.ascontiguousarray(get("L0_attn_hidden_states").reshape(N, C))
    chunks = lambda w: w.reshape(CC, P, -1).transpose(1, 0, 2)
    wq = chunks(get("L0_attn_Wq")).reshape(P, CC, H, R * D)
    wk = chunks(get("L0_attn_Wk")).reshape(P, CC, H, D)
    wv = chunks(get("L0_attn_Wv")).reshape(P, CC, H, D)
    wc = get("L0_attn_Wc").reshape(H, R, D, C).transpose(0, 2, 1, 3).reshape(H, P, R * C)
    per_head = lambda w: w.transpose(2, 0, 1, 3).reshape(H, P, -1)
    wall = np.concatenate([per_head(wq), per_head(wk), per_head(wv), wc], axis=2)
    gate = np.concatenate([get("L0_ffn_w_gate"), get("L0_ffn_sh_gate").reshape(FS // F, F, C)])
    up = np.concatenate([get("L0_ffn_w_up"), get("L0_ffn_sh_up").reshape(FS // F, F, C)])
    gu = np.concatenate([gate[:, 0:P], up[:, 0:P], gate[:, P:], up[:, P:]], axis=1)
    gu = gu.transpose(0, 2, 1).reshape(NX, CC, P, 2 * F).transpose(0, 2, 1, 3)
    dn = np.concatenate([get("L0_ffn_w_down").transpose(0, 2, 1), get("L0_ffn_sh_down").T.reshape(FS // F, F, C)])
    arrays = {
        "xT": x.T.reshape(CC, P, N).transpose(1, 0, 2), "x": x, "wall": wall, "wg": chunks(get("L0_attn_Wg")),
        "gw": chunks(get("L0_ffn_gate_w").T), "bc": get("L0_attn_bc"), "wgu": gu, "wdn": dn, "table": constants(np),
    }
    arrays = {f"in_{k}": np.ascontiguousarray(v) for k, v in arrays.items()}
    nc = bacc.Bacc("TRN2", target_bir_lowering=False, num_devices=1)
    aps = [nc.dram_tensor(k, v.shape, mybir.dt.from_np(v.dtype), kind="ExternalInput").ap() for k, v in arrays.items()]
    out = nc.dram_tensor("out_rows", (N, C), F32, kind="ExternalOutput").ap()
    build(nc, *aps, out)
    result = run(nc, [arrays], core_ids=[0])
    return result.results[0]["out_rows"].reshape(B, T, C)
```

```python
from contextlib import ExitStack
import math

import concourse.bass as bass
from concourse import mybir

F32 = mybir.dt.float32
F32R = mybir.dt.float32r
BF16 = mybir.dt.bfloat16
I32 = mybir.dt.int32
U32 = mybir.dt.uint32
ALU = mybir.AluOpType
ACT = mybir.ActivationFunctionType
AX = mybir.AxisListType

P = 128
B, T, C = 4, 1024, 256
H, R, D = 8, 2, 128
E, F, FS, TOPK, CAP_FACTOR = 64, 176, 352, 6, 2
N = B * T
CC = C // P
TILES = T // P
GROUP = 2 * P
NG = T // GROUP
GATE_OFFSET = 6.906768
SCALE = 1.0 / D ** 0.5
NORM_EPS = 1e-6
LN_EPS = 1e-5
TOPK_EPS = 1e-20
CAP = CAP_FACTOR * ((N * TOPK + E - 1) // E)
CT = CAP // P
VH = D + 2
VW = VH + D
NOWHERE = 1 << 20
NEG = -1e30
FB = F - P
FBO = 64
GU = 2 * P + FBO + FB
KB = FBO + FB
WEIGHTS = CC * GU + 2 * C
MAIN = 512
MT = MAIN // P
OVER_GROUP = 8
ROW = C + E + 4
TOKEN_COL = C + E
NX = E + FS // F

OQ, OK, OV, OC = 0, CC * R * D, CC * (R + 1) * D, CC * (R + 2) * D

K_ID, K_TRI, K_STRICT, K_MASK, K_BASE, K_IOTA, K_END = 0, 128, 256, 384, 640, 704, 768


class Signal:

    def __init__(self, sem, step, once=False):
        self.sem, self.step, self.count = sem, step, 0
        self.once = once


class Queue:

    def __init__(self):
        self.items, self.reached = [], {}
        self.outer, self.told = [], {}

    def put(self, issue, needs=(), tells=None):
        waits = []
        for sig, value in needs:
            if self.reached.get(sig, 0) < value:
                self.reached[sig] = value
                waits.append((sig.sem, value))
        if tells is not None:
            tells.count += tells.step
            self.told[tells] = self.told.get(tells, 0) + tells.step
        self.items.append((waits, issue, tells))
        return [(tells, tells.count)] if tells is not None else []

    def begin_if(self):
        self.outer.append((self.items, self.reached, self.told))
        self.items, self.reached, self.told = [], dict(self.reached), {}

    def end_if(self, needs, condition):
        body, told = self.items, self.told
        self.items, self.reached, self.told = self.outer.pop()
        settled = [(sig.sem, value) for sig, value in needs]
        settled += [(sig.sem, sig.count - n) for sig, n in told.items() if not sig.once]
        finished = [(sig.sem, sig.count) for sig in told if not sig.once]

        def branch(eng):
            with eng.If(condition(eng)):
                Queue.run(eng, body)
                for sem, value in finished:
                    eng.wait_ge(sem, value)
            with eng.Else():
                for sig, n in told.items():
                    if not sig.once:
                        eng.sem_inc(sig.sem, n)
        self.items.append((settled, branch, None))
        for sig, n in told.items():
            self.told[sig] = self.told.get(sig, 0) + n

    @staticmethod
    def run(eng, items):
        for waits, issue, tells in items:
            for sem, value in waits:
                eng.wait_ge(sem, value)
            ins = issue(eng)
            if tells is not None:
                ins.then_inc(tells.sem, tells.step)


def f32(ap):
    return ap.bitcast(F32)


def build(nc, xT, x, wall, wg, gw, bc, wffn, table, out):
    slots = nc.dram_tensor("slots", [E * CAP, ROW], F32).ap()
    y_part = [nc.dram_tensor(f"y_part{i}", [N + CAP, C], F32).ap() for i in range(2)]
    x1_dram = nc.dram_tensor("x1_dram", [N, C], F32).ap()
    x1t_dram = nc.dram_tensor("x1t_dram", [2, P, CC, N], F32).ap()
    decay_dram = nc.dram_tensor("decay_dram", [B, H, T], F32).ap()

    with ExitStack() as ctx:
        def signal(name, step=1, once=False):
            return Signal(ctx.enter_context(nc.semaphore(name)), step, once)

        pe, act, dve, pool, sp = Queue(), Queue(), Queue(), Queue(), Queue()

        def sb(stack, name, shape, dt=F32):
            return stack.enter_context(nc.sbuf_tensor(name, shape, dt))

        bank = [ctx.enter_context(nc.psum_tensor(f"bank{i}", [P, 512], F32)) for i in range(8)]

        tab = sb(ctx, "tab", [P, K_END])
        ones = sb(ctx, "ones", [P, P])
        gw_hi = sb(ctx, "gw_hi", [P, CC, E], F32R)
        gw_lo = sb(ctx, "gw_lo", [P, CC, E], F32R)
        strict_bf = sb(ctx, "strict_bf", [P, P], BF16)
        ones_bf = sb(ctx, "ones_bf", [P, P], BF16)
        ident = tab[:, K_ID:K_ID + P]
        tri = tab[:, K_TRI:K_TRI + P]
        mask = tab[:, K_MASK:K_MASK + GROUP]
        acc = [sb(ctx, f"acc{i}", [P, TILES, C]) for i in range(2)]
        rows = sb(ctx, "rows", [P, TILES, ROW])
        x1t_hi = sb(ctx, "x1t_hi", [P, CC, GROUP], F32R)
        x1t_lo = sb(ctx, "x1t_lo", [P, CC, GROUP], F32R)
        stats = sb(ctx, "stats", [P, TILES, 6])
        mv = sb(ctx, "mv", [P, TILES, 2])
        std = sb(ctx, "std", [P, TILES])
        rstd = sb(ctx, "rstd", [P, TILES])
        row_max = sb(ctx, "row_max", [P, TILES])
        row_sum = sb(ctx, "row_sum", [P, TILES])
        row_rec = sb(ctx, "row_rec", [P, TILES])
        top_sum = sb(ctx, "top_sum", [P, TILES])
        top_rec = sb(ctx, "top_rec", [P, TILES])
        shifted = sb(ctx, "shifted", [P, TILES, E])
        scores = sb(ctx, "scores", [P, TILES, E])
        top8 = sb(ctx, "top8", [P, TILES, 8])
        top8_at = sb(ctx, "top8_at", [P, TILES, 8], U32)
        chosen_at = sb(ctx, "chosen_at", [P, TILES, TOPK])
        onehot = sb(ctx, "onehot", [P, TILES // 4 * TOPK, E])
        chosen = sb(ctx, "chosen", [P, TILES, E])
        chosen_bf = sb(ctx, "chosen_bf", [P, TILES, E], BF16)
        counts = sb(ctx, "counts", [1, E], I32)
        most_f = sb(ctx, "most_f", [1, E // OVER_GROUP])
        most = sb(ctx, "most", [1, E // OVER_GROUP], I32)
        over_flag = sb(ctx, "over_flag", [1, 1])
        taken = sb(ctx, "taken", [P, E])
        slot_of = sb(ctx, "slot_of", [P, TILES, E])
        over = shifted
        slot_f = sb(ctx, "slot_f", [P, TILES, TOPK])
        slot_u = sb(ctx, "slot_u", [P, TILES, TOPK], U32)

        s_const = signal("s_const", 16)
        s_ones = signal("s_ones")
        s_tab = signal("s_tab")
        s_xt_in = signal("s_xt_in", 16)
        s_xt_hi, s_xt_lo = signal("s_xt_hi"), signal("s_xt_lo")
        s_acc_in = [signal(f"s_acc_in{i}", 16) for i in range(2)]
        s_acc0 = signal("s_acc0")
        s_w_in = signal("s_w_in", 16)
        s_w_split = signal("s_w_split")
        s_wc_in, s_wc_split = signal("s_wc_in", 16), signal("s_wc_split")
        s_misc = signal("s_misc")
        s_gate_dve, s_gate_act = signal("s_gate_dve"), signal("s_gate_act")
        s_decay_out = signal("s_decay_out", 16)
        s_decay_in = [signal(f"s_decay_in{i}", 16) for i in range(2)]
        s_mask_dve, s_mask_act = signal("s_mask_dve"), signal("s_mask_act")
        s_vt = signal("s_vt")
        s_qkv_hi, s_qkv_lo = signal("s_qkv_hi"), signal("s_qkv_lo")
        s_scores, s_av = signal("s_scores"), signal("s_av")
        s_sq, s_a32, s_a_hi, s_a_lo = signal("s_sq"), signal("s_a32"), signal("s_a_hi"), signal("s_a_lo")
        s_off, s_num, s_y = signal("s_off"), signal("s_num"), signal("s_y")
        s_yt_hi, s_yt_lo = signal("s_yt_hi"), signal("s_yt_lo")
        s_acc = signal("s_acc")
        s_ln, s_ln_act = signal("s_ln"), signal("s_ln_act")
        s_rows_pool = signal("s_rows_pool")
        s_x1t_hi, s_x1t_lo = signal("s_x1t_hi"), signal("s_x1t_lo")
        s_x1_out = signal("s_x1_out", 16)
        s_x1t_out = signal("s_x1t_out", 16)
        s_route, s_route_act = signal("s_route"), signal("s_route_act")
        s_init = signal("s_init")
        s_slots0 = signal("s_slots0", 16)
        s_scatter = signal("s_scatter", 16)

        misc = {"next": 0, "free": [[], []]}
        put_off = []

        def catch_up():
            while put_off:
                put_off.pop(0)[1]()

        def take_misc():
            i = misc["next"]
            misc["next"] = 1 - i
            if any(j == i for j, _ in put_off):
                catch_up()
            return i, bank[6 + i], misc["free"][i]

        def three_passes(put_mm, a_hi, a_lo, b_hi, b_lo):
            put_mm(a_hi, b_hi)
            put_mm(a_hi, b_lo)
            put_mm(a_lo, b_hi)

        def product(dst, terms, needs, tells, first=True, last=True):
            mms = []
            for a_hi, a_lo, b_hi, b_lo in terms:
                three_passes(lambda a, b: mms.append((a, b)), a_hi, a_lo, b_hi, b_lo)
            done = []
            for i, (a, b) in enumerate(mms):
                start, stop = first and i == 0, last and i == len(mms) - 1
                done = pe.put(lambda e, a=a, b=b, start=start, stop=stop: e.matmul(
                    dst, a, b, start=start, stop=stop, skip_group_check=True),
                    needs if i == 0 else (), tells if i == len(mms) - 1 else None)
            return done

        act.put(lambda e: e.dma_start(tab[:, :], table), (), s_const)
        tok, x1_stored = {}, {}
        with ExitStack() as att:
            xt_hi = sb(att, "xt_hi", [P, CC, T], F32R)
            xt_lo = sb(att, "xt_lo", [P, CC, T], F32R)
            w_raw = sb(att, "w_raw", [P, OC])
            xt_raw = w_raw[:, :].rearrange("p (c t) -> p c t", c=CC)
            wc_raw = sb(att, "wc_raw", [P, R, C])
            w_hi = [sb(att, f"w_hi{i}", [P, OC], F32R) for i in range(2)]
            w_lo = [sb(att, f"w_lo{i}", [P, OC], F32R) for i in range(2)]
            wc_hi = [sb(att, f"wc_hi{i}", [P, R, C], F32R) for i in range(2)]
            wc_lo = [sb(att, f"wc_lo{i}", [P, R, C], F32R) for i in range(2)]
            q_hi = [sb(att, f"q_hi{i}", [P, R, T], F32R) for i in range(2)]
            q_lo = [sb(att, f"q_lo{i}", [P, R, T], F32R) for i in range(2)]
            k_hi = [sb(att, f"k_hi{i}", [P, T], F32R) for i in range(2)]
            k_lo = [sb(att, f"k_lo{i}", [P, T], F32R) for i in range(2)]
            v_pair = [sb(att, f"v_pair{i}", [P, TILES, VW], F32R) for i in range(2)]
            vt = sb(att, "vt", [P, 512])
            wg_raw = sb(att, "wg_raw", [P, CC, H])
            wg_hi = sb(att, "wg_hi", [P, CC, H], F32R)
            wg_lo = sb(att, "wg_lo", [P, CC, H], F32R)
            gw_raw = sb(att, "gw_raw", [P, CC, E])
            bc_all = sb(att, "bc_all", [P, C])
            zg = sb(att, "zg", [P, TILES, H])
            zn = sb(att, "zn", [P, TILES, H])
            log_g = sb(att, "log_g", [P, TILES, H])
            local = [sb(att, f"local{i}", [P, TILES, H]) for i in range(2)]
            f_t = [sb(att, f"f_t{i}", [P, TILES, H]) for i in range(2)]
            ref = sb(att, "ref", [P, NG, H])
            whole = sb(att, "whole", [P, TILES, H])
            c_arg = sb(att, "c_arg", [P, NG * (NG - 1), H])
            c_s = [sb(att, f"c_s{i}", [P, NG * (NG - 1), H]) for i in range(2)]
            decay_rows = sb(att, "decay_rows", [H, T])
            decay_all = [sb(att, f"decay_all{i}", [P, GROUP]) for i in range(2)]
            em = [sb(att, f"em{i}", [P, GROUP + P]) for i in range(2)]
            ln_scale2 = sb(att, "ln_scale2", [P, 1])
            ln_scale = sb(att, "ln_scale", [P, 1])
            a32 = [sb(att, f"a32_{i}", [P, R, GROUP]) for i in range(2)]
            a_hi = [sb(att, f"a_hi{i}", [P, R, GROUP], F32R) for i in range(4)]
            a_lo = [sb(att, f"a_lo{i}", [P, R, GROUP], F32R) for i in range(4)]
            sums = sb(att, "sums", [P, 2 * R, VW])
            nrm = sb(att, "nrm", [P, 2 * R])
            rec = sb(att, "rec", [P, 2 * R])
            y_n = [sb(att, f"y_n{i}", [P, 2 * R, D]) for i in range(2)]
            yt_hi = sb(att, "yt_hi", [P, R, GROUP], F32R)
            yt_lo = sb(att, "yt_lo", [P, R, GROUP], F32R)
            slot0 = acc[1][:, :, :].rearrange("p j c -> p (j c)")[:, 0:CT * ROW].rearrange("p (j c) -> p j c", c=ROW)

            sp.put(lambda e: e.dma_start(wg_raw[:, :, :], wg), (), s_const)
            sp.put(lambda e: e.dma_start(gw_raw[:, :, :], gw), (), s_const)
            const_in = sp.put(lambda e: e.dma_start(bc_all[:, :], bc.partition_broadcast(P)), (), s_const)
            pool.put(lambda e: e.memset(ones[:, :], 1.0), (), s_ones)
            pool.put(lambda e: e.memset(ones_bf[:, :], 1.0), (), s_ones)
            pool.put(lambda e: e.memset(taken[:, :], 0.0), (), s_ones)
            pool.put(lambda e: e.memset(rows[:, :, TOKEN_COL + 1:ROW], 0.0), (), s_ones)
            pool.put(lambda e: e.memset(ln_scale2[:, :], 2.0 * math.log(SCALE)), (), s_ones)
            pool.put(lambda e: e.memset(ln_scale[:, :], math.log(SCALE)), (), s_ones)
            pool.put(lambda e: e.memset(slot0[:, :, 0:TOKEN_COL], 0.0), (), s_init)
            pool.put(lambda e: e.memset(slot0[:, :, TOKEN_COL + 1:ROW], 0.0), (), s_init)
            slot0_ready = pool.put(lambda e: e.iota(slot0[:, :, TOKEN_COL].bitcast(I32), pattern=[[P, CT]], base=N,
                                                    channel_multiplier=1), (), s_init)
            for i in range(2):
                dve.put(lambda e, i=i: e.memset(f32(v_pair[i][:, :, D:D + 1]), 1.0), (), s_tab)
                dve.put(lambda e, i=i: e.memset(f32(v_pair[i][:, :, D + 1:VH]), 0.0), (), s_tab)
            ones_ready = [(s_ones, s_ones.count)]
            dve.put(lambda e: e.tensor_copy(strict_bf[:, :], tab[:, K_STRICT:K_STRICT + P]), const_in, s_tab)
            dve.put(lambda e: e.tensor_copy(wg_hi[:, :, :], wg_raw[:, :, :]), (), s_tab)
            t = dve.put(lambda e: e.tensor_copy(gw_hi[:, :, :], gw_raw[:, :, :]), (), s_tab)
            dve.put(lambda e: e.tensor_tensor(wg_lo[:, :, :], wg_raw[:, :, :], f32(wg_hi[:, :, :]), ALU.subtract), t, s_tab)
            tab_ready = dve.put(lambda e: e.tensor_tensor(gw_lo[:, :, :], gw_raw[:, :, :], f32(gw_hi[:, :, :]),
                                                          ALU.subtract), (), s_tab)

            def prepare_batch(b):
                i = b % 2
                for half in range(2):
                    hs = slice(half * T // 2, (half + 1) * T // 2)
                    loaded = sp.put(lambda e, half=half: e.dma_start(
                        xt_raw, xT[:, :, b * T + half * T // 2:b * T + (half + 1) * T // 2]),
                        tok.get("xt_lo", []) + tok.get("w_split", []), s_xt_in)
                    hi = act.put(lambda e, hs=hs: e.activation(xt_hi[:, :, hs], xt_raw, ACT.Copy),
                                 loaded + tok.get("qkv_mm", []), s_xt_hi)
                    lo = dve.put(lambda e, hs=hs: e.tensor_tensor(xt_lo[:, :, hs], xt_raw,
                                                                  f32(xt_hi[:, :, hs]), ALU.subtract), hi, s_xt_lo)
                    tok["xt_lo"] = lo
                tok["xt"] = hi + lo
                got = sp.put(lambda e: e.dma_start(acc[i][:, :, :], x[b * T:(b + 1) * T, :].rearrange(
                    "(j p) c -> p j c", p=P)), tok.get(("ln", b - 2), []) + ([(s_slots0, s_slots0.count)] if b == 1 else []),
                             s_acc_in[i])
                tok["acc0", b] = pool.put(lambda e: e.tensor_tensor(
                    acc[i][:, :, :], acc[i][:, :, :], bc_all[:, :].unsqueeze(1).to_broadcast([P, TILES, C]), ALU.add),
                    got + const_in, s_acc0)

            def gates(b):
                i = b % 2
                g = s_gate_dve
                for half in range(2):
                    hs = slice(half * T // 2, (half + 1) * T // 2)
                    m, ps, free = take_misc()
                    mm = product(ps[0:H, :], [(wg_hi[:, c, :], wg_lo[:, c, :], xt_hi[:, c, hs], xt_lo[:, c, hs])
                                              for c in range(CC)], tok["xt"] + tab_ready + free, s_misc)
                    t = misc["free"][m] = dve.put(lambda e, ps=ps, hs=hs: e.tensor_copy(decay_rows[:, hs], ps[0:H, :]),
                                                  mm + tok.get("decay_out", []), g)
                    yield
                m, ps, free = take_misc()
                g_ps = ps[:, 0:TILES * H].rearrange("p (j h) -> p j h", h=H)
                for j in range(TILES):
                    mm = pe.put(lambda e, j=j: e.transpose(g_ps[:, j, :], decay_rows[:, j * P:(j + 1) * P],
                                                           ident[0:H, 0:H]), t + free, s_misc if j == TILES - 1 else None)
                t = dve.put(lambda e: e.tensor_scalar(zg[:, :, :], g_ps, GATE_OFFSET, None, ALU.add), mm, g)
                misc["free"][m] = t
                t = dve.put(lambda e: e.scalar_tensor_tensor(out=zn[:, :, :], in0=zg[:, :, :], scalar=-1.0,
                                                             in1=zg[:, :, :], op0=ALU.mult, op1=ALU.min), t, g)
                t = act.put(lambda e: e.activation(zn[:, :, :], zn[:, :, :], ACT.Exp), t, s_gate_act)
                t = act.put(lambda e: e.activation(zn[:, :, :], zn[:, :, :], ACT.Ln, bias=ones[:, 0:1]),
                            t + ones_ready, s_gate_act)
                t = dve.put(lambda e: e.scalar_tensor_tensor(out=log_g[:, :, :], in0=zg[:, :, :], scalar=0.0,
                                                             in1=zn[:, :, :], op0=ALU.min, op1=ALU.subtract), t, g)
                yield
                m, ps, free = take_misc()
                loc = ps[:, 0:TILES * H].rearrange("p (j h) -> p j h", h=H)
                pair = ps[:, 0:TILES * H].rearrange("p (g k h) -> p g k h", k=2, h=H)
                lg_pair = log_g[:, :, :].rearrange("p (g k) h -> p g k h", k=2)
                tot = ps[:, TILES * H:2 * TILES * H].rearrange("p (g k h) -> p g k h", k=2, h=H)
                pe.put(lambda e: e.matmul(loc, tri, log_g[:, :, :], start=True, stop=False, skip_group_check=True),
                       t + free)
                pe.put(lambda e: e.matmul(pair[:, :, 1, :], ones[:, :], lg_pair[:, :, 0, :], start=False, stop=True,
                                          skip_group_check=True))
                mm = pe.put(lambda e: e.matmul(tot, ones[:, :], log_g[:, :, :], start=False, stop=True,
                                               skip_group_check=True), (), s_misc)
                heads_past = tok.get(("heads", b - 2), [])
                dve.put(lambda e: e.tensor_copy(local[i][:, :, :], loc), mm + heads_past, g)
                dve.put(lambda e: e.memset(ref[:, 0, :], 0.0), (), g)
                t = dve.put(lambda e: e.tensor_tensor(ref[:, 1, :], tot[:, 0, 0, :], ref[:, 0, :], ALU.add),
                            [(g, g.count)], g)
                t = dve.put(lambda e: e.tensor_tensor(ref[:, 1, :], tot[:, 0, 1, :], ref[:, 1, :], ALU.add), t, g)
                for k in range(2, NG):
                    t = dve.put(lambda e, k=k: e.tensor_tensor(ref[:, k, :], tot[:, k - 1, 0, :], ref[:, k - 1, :],
                                                               ALU.add), t, g)
                    t = dve.put(lambda e, k=k: e.tensor_tensor(ref[:, k, :], tot[:, k - 1, 1, :], ref[:, k, :],
                                                               ALU.add), t, g)
                misc["free"][m] = t
                t = dve.put(lambda e: e.tensor_tensor(
                    whole[:, :, :].rearrange("p (g k) h -> p g k h", k=2),
                    local[i][:, :, :].rearrange("p (g k) h -> p g k h", k=2),
                    ref[:, :, :].unsqueeze(2).to_broadcast([P, NG, 2, H]), ALU.add), t, g)
                for k in range(1, NG):
                    t = dve.put(lambda e, k=k: e.tensor_tensor(
                        c_arg[:, k * (k - 1):k * (k + 1), :],
                        ref[:, k, :].unsqueeze(1).to_broadcast([P, 2 * k, H]), whole[:, 0:2 * k, :],
                        ALU.subtract), t + [(s_gate_act, s_gate_act.count)], g)
                t = act.put(lambda e: e.activation(c_s[i][:, :, :], c_arg[:, :, :], ACT.Exp,
                                                   bias=ln_scale[:, :], scale=0.5), t + heads_past, s_gate_act)
                t = act.put(lambda e: e.activation(f_t[i][:, :, :], local[i][:, :, :], ACT.Exp), (), s_gate_act)
                yield
                for half in range(2):
                    m, ps, free = take_misc()
                    gs = range(half * NG // 2, (half + 1) * NG // 2)
                    for n, k in enumerate(gs):
                        o = ps[0:H, n * GROUP:(n + 1) * GROUP]
                        pe.put(lambda e, o=o, k=k, n=n: e.matmul(o[:, 0:P], log_g[:, 2 * k, :], tri, start=(n == 0),
                                                                 stop=False, skip_group_check=True), free)
                        pe.put(lambda e, o=o, k=k: e.matmul(o[:, P:GROUP], log_g[:, 2 * k, :], ones[:, :], start=False,
                                                            stop=False, skip_group_check=True))
                        mm = pe.put(lambda e, o=o, k=k: e.matmul(o[:, P:GROUP], log_g[:, 2 * k + 1, :], tri,
                                                                 start=False, stop=True, skip_group_check=True),
                                    (), s_misc if n == 1 else None)
                    t = dve.put(lambda e, ps=ps, half=half: e.tensor_copy(
                        decay_rows[:, half * 512:(half + 1) * 512], ps[0:H, :]), mm + tok.get("decay_out", []), g)
                    misc["free"][m] = t
                tok["gates", b] = [(s_gate_dve, s_gate_dve.count), (s_gate_act, s_gate_act.count)]
                tok["decay_out"] = sp.put(lambda e: e.dma_start(decay_dram[b], decay_rows[:, :]), t, s_decay_out)
                tok["decay_out", b] = tok["decay_out"]
                yield

            def load_decay(n, k):
                b, h = divmod(n, H)
                tok["decay", n, k] = sp.put(lambda e: e.dma_start(
                    decay_all[k % 2][:, :], decay_dram[b, h:h + 1, k * GROUP:(k + 1) * GROUP].to_broadcast([P, GROUP])),
                    tok["decay_out", b] + tok.get(("em_arg", k % 2), []), s_decay_in[k % 2])

            def decay_args(n, k):
                b, h = divmod(n, H)
                i, bi = k % 2, b % 2
                free = tok.get(("em_read", i), [])
                dve.put(lambda e: e.scalar_tensor_tensor(
                    out=em[i][:, 0:GROUP], in0=decay_all[i][:, :],
                    scalar=local[bi][:, 2 * k, h:h + 1], in1=mask, op0=ALU.subtract, op1=ALU.min),
                    tok["decay", n, k] + free + tok["gates", b], s_mask_dve)
                t = dve.put(lambda e: e.scalar_tensor_tensor(
                    out=em[i][:, GROUP:GROUP + P], in0=decay_all[i][:, P:GROUP],
                    scalar=local[bi][:, 2 * k + 1, h:h + 1], in1=mask[:, 0:P], op0=ALU.subtract, op1=ALU.min),
                    (), s_mask_dve)
                tok["em_arg", i] = t

            def decay_matrices(n, k):
                i, t = k % 2, tok["em_arg", k % 2]
                tok["em", n, k] = act.put(lambda e: e.activation(em[i][:, :], em[i][:, :], ACT.Exp,
                                                                 bias=ln_scale2[:, :]), t, s_mask_act)

            def load_qkv_weights(n):
                h, i = n % H, n % 2
                raw = w_raw[:, :] if n else sums[:, :, :].rearrange("p k v -> p (k v)")[:, 0:OC]
                need = tok.get("w_split", []) + tok["xt_lo"] if n else []
                got = sp.put(lambda e: e.dma_start(raw, wall[h, :, 0:OC]), need, s_w_in)
                hi = pool.put(lambda e: e.tensor_copy(w_hi[i][:, :], raw), got + tok.get(("qkv_mm", n - 2), []),
                              s_w_split)
                tok["w_split"] = tok["w", n] = pool.put(lambda e: e.tensor_tensor(
                    w_lo[i][:, :], raw, f32(w_hi[i][:, :]), ALU.subtract), hi, s_w_split)

            def load_out_weights(n):
                h, i = n % H, n % 2
                raw = wc_raw[:, :, :]
                got = sp.put(lambda e: e.dma_start(raw, wall[h, :, OC:].rearrange("p (r m) -> p r m", r=R)),
                             tok.get("wc_split", []), s_wc_in)
                hi = pool.put(lambda e: e.tensor_copy(wc_hi[i][:, :, :], raw), got + tok.get(("proj", n - 2), []),
                              s_wc_split)
                tok["wc_split"] = tok["wc", n] = pool.put(lambda e: e.tensor_tensor(
                    wc_lo[i][:, :, :], raw, f32(wc_hi[i][:, :, :]), ALU.subtract), hi, s_wc_split)

            def weights(n, hi):
                w = (w_hi if hi else w_lo)[n % 2]
                return [w[:, o:z].rearrange("p (c m) -> p c m", c=CC) for o, z in ((OQ, OK), (OK, OV), (OV, OC))]

            def qkv_tasks(n):
                i = n % 2
                hi, lo = weights(n, True), weights(n, False)
                tasks = []

                def split(ps, m, mm, dst_hi, dst_lo, src, what):
                    t = act.put(lambda e: e.activation(dst_hi, src, ACT.Copy), mm + tok.get(("av", n - 2), []), s_qkv_hi)
                    tok["qkv_mm"] = tok["qkv_mm", n] = mm

                    def later():
                        t2 = dve.put(lambda e: e.tensor_tensor(dst_lo, src, f32(dst_hi), ALU.subtract), mm + t, s_qkv_lo)
                        misc["free"][m] = t + t2
                        tok[what] = t + t2
                    put_off.append((m, later))

                def column(which, r, tc):
                    def run():
                        m, ps, free = take_misc()
                        cols = slice(r * D, (r + 1) * D)
                        mm = product(ps[:, :], [(hi[which][:, c, cols], lo[which][:, c, cols],
                                                 xt_hi[:, c, tc * 512:(tc + 1) * 512],
                                                 xt_lo[:, c, tc * 512:(tc + 1) * 512]) for c in range(CC)],
                                     free + tok["w", n] + tok["xt"], s_misc)
                        dst = [(q[i][:, r, tc * 512:(tc + 1) * 512] if which == 0 else k[i][:, tc * 512:(tc + 1) * 512])
                               for q, k in ((q_hi, k_hi), (q_lo, k_lo))]
                        split(ps, m, mm, dst[0], dst[1], ps[:, :], ("qk", n, tc))
                    return run

                def value(tc):
                    m, ps, free = take_misc()
                    mm = product(ps[:, :], [(hi[2][:, c, :], lo[2][:, c, :], xt_hi[:, c, tc * 512:(tc + 1) * 512],
                                             xt_lo[:, c, tc * 512:(tc + 1) * 512]) for c in range(CC)],
                                 free + tok["w", n] + tok["xt"], s_misc)
                    tok["qkv_mm"] = tok["qkv_mm", n] = mm
                    misc["free"][m] = tok["vt"] = act.put(lambda e: e.activation(vt[:, :], ps[:, :], ACT.Copy),
                                                          mm + tok.get("vt_read", []), s_vt)

                def turn_value(tc):
                    m, ps, free = take_misc()
                    for j in range(4):
                        mm = pe.put(lambda e, j=j: e.transpose(ps[:, j * P:(j + 1) * P], vt[:, j * P:(j + 1) * P], ident),
                                    tok["vt"] + free, s_misc if j == 3 else None)
                    tok["vt_read"] = mm
                    js = slice(4 * tc, 4 * tc + 4)
                    split(ps, m, mm, v_pair[i][:, js, 0:D], v_pair[i][:, js, VH:VW],
                          ps[:, :].rearrange("p (j d) -> p j d", d=D), ("v", n, tc))

                for tc in range(T // 512):
                    tasks += [column(1, 0, tc), column(0, 0, tc), lambda tc=tc: value(tc), column(0, 1, tc),
                              lambda tc=tc: turn_value(tc)]
                return tasks

            def fill_dram(n, parts):
                stores = [(slots[ex * CAP:(ex + 1) * CAP, :], slot0[:, :, :]) for ex in range(E)]
                stores += [(y_part[1][lo:min(lo + CAP, N + CAP), :], slot0[:, 0:min(CAP, N + CAP - lo) // P, 0:C])
                           for lo in range(0, N + CAP, CAP)]
                stores += [(y_part[0][N:N + CAP, :], slot0[:, :, 0:C])]
                for dst, src in stores[n * len(stores) // parts:(n + 1) * len(stores) // parts]:
                    sp.put(lambda e, dst=dst, src=src: e.dma_start(dst.rearrange("(j p) c -> p j c", p=P), src),
                           slot0_ready, s_slots0)

            units = []
            for n in range(B * H):
                for g in range(NG):
                    for s in range(2 * g + 2):
                        units.append((n, g, s))
            av_done, made = {}, {}

            def score_tile(u):
                n, g, s = units[u]
                i, ps = n % 2, bank[u % 2]
                t0 = P if s == 2 * g + 1 else 0
                w = GROUP - t0
                dst = ps[:, 0:R * w].rearrange("p (r t) -> p r t", r=R)
                qs = slice(g * GROUP + t0, (g + 1) * GROUP)
                ks = slice(s * P, (s + 1) * P)
                return product(dst, [(k_hi[i][:, ks], k_lo[i][:, ks], q_hi[i][:, :, qs], q_lo[i][:, :, qs])],
                               tok["qk", n, max(s, 2 * g + 1) // 4] + made.get(("read", u - 2), []), s_scores)

            def square(u, mm):
                n, g, s = units[u]
                b, h = divmod(n, H)
                bi = b % 2
                w = P if s == 2 * g + 1 else GROUP
                src = bank[u % 2][:, 0:R * w].rearrange("p (r t) -> p r t", r=R)
                raw = a32[u % 2][:, :, 0:w]
                raw_free = made.get(u - 2, [])
                if s < 2 * g:
                    scale = c_s[bi][:, g * (g - 1) + s, h:h + 1]
                    t = act.put(lambda e: e.activation(raw, src, ACT.Square, scale=scale),
                                mm + raw_free + tok["gates", b], s_sq)
                    made["read", u] = t
                else:
                    t = act.put(lambda e: e.activation(raw, src, ACT.Square), mm + raw_free, s_sq)
                    made["read", u] = t
                    decay = em[g % 2][:, 0:GROUP] if s == 2 * g else em[g % 2][:, GROUP:GROUP + P]
                    t = dve.put(lambda e: e.tensor_tensor(raw, raw, decay.unsqueeze(1).to_broadcast([P, R, w]),
                                                          ALU.mult), t + tok["em", n, g], s_a32)
                    tok["em_read", g % 2] = t
                made["a32", u] = t

            def pair_a(u):
                n, g, s = units[u]
                w = P if s == 2 * g + 1 else GROUP
                raw = a32[u % 2][:, :, 0:w]
                hi, lo = a_hi[u % 4][:, :, 0:w], a_lo[u % 4][:, :, 0:w]
                free = av_done.get(u - 4, [])
                t = act.put(lambda e: e.activation(hi, raw, ACT.Copy), made["a32", u] + free, s_a_hi)
                t2 = dve.put(lambda e: e.tensor_tensor(lo, raw, f32(hi), ALU.subtract), t + free, s_a_lo)
                made[u] = t + t2

            sum_free = [[] for _ in range(2 * R)]

            def value_product(u):
                n, g, s = units[u]
                i, i4 = n % 2, u % 4
                tts = [1] if s == 2 * g + 1 else [0, 1]
                t_off = P if s == 2 * g + 1 else 0
                for tt in tts:
                    first = s in (0, 2 * g)
                    last = s == 2 * g - 1 or s == 2 * g + tt
                    for r in range(R):
                        k = tt * R + r
                        cols = slice(tt * P - t_off, (tt + 1) * P - t_off)
                        pe.put(lambda e, k=k, r=r, cols=cols, first=first: e.matmul(
                            bank[2 + k][:, 0:VW], a_hi[i4][:, r, cols], v_pair[i][:, s, :], start=first, stop=False,
                            skip_group_check=True), made[u] + tok["v", n, s // 4] + (sum_free[k] if first else []))
                        done = pe.put(lambda e, k=k, r=r, cols=cols, last=last: e.matmul(
                            bank[2 + k][:, 0:VH], a_lo[i4][:, r, cols], v_pair[i][:, s, 0:VH], start=False, stop=last,
                            skip_group_check=True), (), s_av if last or (tt, r) == (tts[-1], R - 1) else None)
                        if last:
                            tok["sum", k] = done
                av_done[u] = tok["av", n] = done
                if s == 2 * g - 1:
                    for k in range(2 * R):
                        t = act.put(lambda e, k=k: e.activation(sums[:, k, :], bank[2 + k][:, 0:VW], ACT.Copy),
                                    tok["sum", k] + tok.get("sums_read", []), s_off)
                        sum_free[k] = t
                    tok["off"] = t

            def merge(n, g, tt):
                b, h = divmod(n, H)
                bi = b % 2
                for k in range(tt * R, (tt + 1) * R):
                    dg = bank[2 + k][:, 0:VW]
                    if g == 0:
                        t = act.put(lambda e, k=k, dg=dg: e.activation(sums[:, k, :], dg, ACT.Copy),
                                    tok["sum", k] + tok.get("sums_read", []), s_off)
                    else:
                        t = dve.put(lambda e, k=k, dg=dg: e.scalar_tensor_tensor(
                            out=sums[:, k, :], in0=sums[:, k, :], scalar=f_t[bi][:, 2 * g + k // R, h:h + 1],
                            in1=dg, op0=ALU.mult, op1=ALU.add), tok["sum", k] + tok["off"] + tok["gates", b], s_num)
                    sum_free[k] = t
                tok["num", tt] = tok["num"] = t

            def normalise(n, g):
                t = tok["num", 0] + tok["num", 1]
                dve.put(lambda e: e.tensor_scalar(nrm[:, :], sums[:, :, D], NORM_EPS, None, ALU.add), t, s_y)
                y = y_n[g % 2]
                t = dve.put(lambda e: e.tensor_tensor(y[:, :, :], sums[:, :, 0:D], sums[:, :, VH:VW], ALU.add),
                            t + tok.get(("y_read", g % 2), []), s_y)
                tok["sums_read"] = t
                t = dve.put(lambda e: e.reciprocal(rec[:, :], nrm[:, :]), [(s_y, s_y.count - 1)], s_y)
                return dve.put(lambda e: e.tensor_tensor(
                    y[:, :, :], y[:, :, :], rec[:, :].unsqueeze(2).to_broadcast([P, 2 * R, D]), ALU.mult), t, s_y)

            def turn(n, g, normalised):
                m, ps, free = take_misc()
                for tt in range(2):
                    for r in range(R):
                        mm = pe.put(lambda e, tt=tt, r=r, ps=ps: e.transpose(
                            ps[:, r * GROUP + tt * P:r * GROUP + (tt + 1) * P], y_n[g % 2][:, tt * R + r, :], ident),
                            normalised + free + const_in, s_misc if (tt, r) == (1, R - 1) else None)
                tok["y_read", g % 2] = mm
                src = ps[:, :].rearrange("p (r t) -> p r t", r=R)
                t = act.put(lambda e: e.activation(yt_hi[:, :, :], src, ACT.Copy), mm + tok.get("yt_read", []), s_yt_hi)
                ready = []

                def later():
                    t2 = dve.put(lambda e: e.tensor_tensor(yt_lo[:, :, :], src, f32(yt_hi[:, :, :]), ALU.subtract),
                                 mm + t, s_yt_lo)
                    misc["free"][m] = t + t2
                    ready.extend(t + t2)
                put_off.append((m, later))
                return ready

            def project(n, g, ready):
                b = n // H
                hi, lo = wc_hi[n % 2], wc_lo[n % 2]
                m, ps, free = take_misc()
                for tt in range(2):
                    ts = slice(tt * P, (tt + 1) * P)
                    mm = product(ps[:, tt * C:(tt + 1) * C], [(yt_hi[:, r, ts], yt_lo[:, r, ts], hi[:, r, :], lo[:, r, :])
                                                              for r in range(R)],
                                 ready + free + tok["wc", n], s_misc if tt else None, first=(tt == 0))
                tok["yt_read"] = tok["proj", n] = mm
                part = acc[b % 2][:, 2 * g:2 * g + 2, :]

                def later():
                    t = dve.put(lambda e: e.tensor_tensor(part, ps[:, :].rearrange("p (j c) -> p j c", c=C), part, ALU.add),
                                mm + tok["acc0", b] + tok.get(("acc", b, g), []), s_acc)
                    misc["free"][m] = tok["acc", b, g] = tok["acc", b] = t
                put_off.append((m, later))

            def route(b):
                i = b % 2
                st = {}
                L, Q = s_ln, s_route
                st["rows_free"] = tok.get("rows_read", [])

                def layer_norm():
                    for j in range(TILES):
                        dve.put(lambda e, j=j: e.bn_stats(stats[:, j, :], acc[i][:, j, :]), tok["acc", b], L)
                        if j % 2:
                            yield
                    t = [(L, L.count)]
                    for j in range(TILES):
                        t = dve.put(lambda e, j=j: e.bn_aggr(mv[:, j, :], stats[:, j, :]), t, L)
                    t = dve.put(lambda e: e.tensor_scalar(std[:, :], mv[:, :, 1], LN_EPS, None, ALU.add), t, L)
                    t = act.put(lambda e: e.activation(std[:, :], std[:, :], ACT.Sqrt), t, s_ln_act)
                    yield
                    t = dve.put(lambda e: e.reciprocal(rstd[:, :], std[:, :]), t, L)
                    for j in range(TILES):
                        t = dve.put(lambda e, j=j: e.tensor_scalar(rows[:, j, 0:C], acc[i][:, j, :], mv[:, j, 0:1],
                                                                   rstd[:, j:j + 1], ALU.subtract, ALU.mult),
                                    t + st["rows_free"], L)
                        if j % 2:
                            yield
                    st["x1"] = tok["ln", b] = t
                    sp.put(lambda e: e.dma_start(x1_dram[b * T:(b + 1) * T, :].rearrange("(j p) c -> p j c", p=P),
                                                 rows[:, :, 0:C]), t, s_x1_out)
                    x1_stored[b] = [(s_x1_out, s_x1_out.count), (s_x1t_out, s_x1t_out.count + 16 * 2 * NG)]
                    st["token"] = pool.put(lambda e: e.iota(rows[:, :, TOKEN_COL].bitcast(I32), pattern=[[P, TILES]],
                                                            base=b * T, channel_multiplier=1),
                                           st["rows_free"], s_rows_pool)

                def turn_x1():
                    for k in range(NG):
                        st["pair"] = turn_x1_group(k)
                        yield
                        logit_group(k, st["pair"])
                        yield

                def turn_x1_group(k):
                    m, ps, free = take_misc()
                    for jj in range(2):
                        for c in range(CC):
                            mm = pe.put(lambda e, jj=jj, c=c: e.transpose(
                                ps[:, c * GROUP + jj * P:c * GROUP + (jj + 1) * P],
                                rows[:, 2 * k + jj, c * P:(c + 1) * P], ident),
                                st["x1"] + free, s_misc if (jj, c) == (1, CC - 1) else None)
                    src = ps[:, :].rearrange("p (c t) -> p c t", c=CC)
                    hi, lo = x1t_hi, x1t_lo
                    t = act.put(lambda e: e.activation(hi[:, :, :], src, ACT.Copy),
                                mm + tok.get("x1t_read", []), s_x1t_hi)
                    t2 = dve.put(lambda e: e.tensor_tensor(lo[:, :, :], src, f32(hi[:, :, :]),
                                                           ALU.subtract), mm + t, s_x1t_lo)
                    misc["free"][m] = t + t2
                    ts = slice(b * T + k * GROUP, b * T + (k + 1) * GROUP)
                    sp.put(lambda e: e.dma_start(x1t_dram[0, :, :, ts], f32(hi[:, :, :])), t, s_x1t_out)
                    stored = sp.put(lambda e: e.dma_start(x1t_dram[1, :, :, ts], f32(lo[:, :, :])), t2,
                                    s_x1t_out)
                    return t, t2, stored

                def logit_group(k, pair):
                    t, t2, stored = pair
                    hi, lo = x1t_hi, x1t_lo
                    m, ps_lg, free = take_misc()
                    lg = ps_lg[:, 0:2 * E].rearrange("p (j e) -> p j e", e=E)
                    for jj in range(2):
                        js = slice(jj * P, (jj + 1) * P)
                        mm = product(lg[:, jj, :], [(hi[:, c, js], lo[:, c, js], gw_hi[:, c, :], gw_lo[:, c, :])
                                                    for c in range(CC)],
                                     t + t2 + free + tab_ready, s_misc if jj else None, first=(jj == 0))
                    tok["x1t_read"] = stored + mm
                    t = dve.put(lambda e: e.tensor_copy(shifted[:, 2 * k:2 * k + 2, :], lg), mm, s_route)
                    misc["free"][m] = t
                    st["logit"] = t

                def logits():
                    lg = shifted[:, :, :]
                    mm = st["logit"]
                    wide = lambda v: v[:, :].unsqueeze(2).to_broadcast([P, TILES, E])
                    t = dve.put(lambda e: e.tensor_reduce(row_max[:, :], lg, AX.X, ALU.max), mm, Q)
                    t = dve.put(lambda e: e.tensor_tensor(shifted[:, :, :], lg, wide(row_max), ALU.subtract), t, Q)
                    t = act.put(lambda e: e.activation(shifted[:, :, :], shifted[:, :, :], ACT.Exp), t, s_route_act)
                    yield
                    t = dve.put(lambda e: e.tensor_reduce(row_sum[:, :], shifted[:, :, :], AX.X, ALU.add), t, Q)
                    t = dve.put(lambda e: e.reciprocal(row_rec[:, :], row_sum[:, :]), t, Q)
                    st["t"] = dve.put(lambda e: e.tensor_tensor(scores[:, :, :], shifted[:, :, :], wide(row_rec),
                                                                ALU.mult), t, Q)
                    yield

                def top():
                    t = st["t"]
                    for j in range(TILES):
                        dve.put(lambda e, j=j: e.max(out=top8[:, j, :], in_=scores[:, j, :]), t, Q)
                    t = [(Q, Q.count)]
                    yield
                    for j in range(TILES):
                        dve.put(lambda e, j=j: e.max_index(out=top8_at[:, j, :], in_max=top8[:, j, :],
                                                           in_values=scores[:, j, :]), t, Q)
                    t = [(Q, Q.count)]
                    yield
                    t = dve.put(lambda e: e.tensor_copy(chosen_at[:, :, :], top8_at[:, :, 0:TOPK]), t, Q)
                    q4 = TILES // 4
                    iota = tab[:, K_IOTA:K_IOTA + E].unsqueeze(1).to_broadcast([P, q4 * TOPK, E])
                    for q in range(4):
                        js = slice(q * q4, (q + 1) * q4)
                        t = dve.put(lambda e, js=js: e.tensor_tensor(
                            onehot[:, :, :], chosen_at[:, js, :].rearrange("p j k -> p (j k)").unsqueeze(2)
                            .to_broadcast([P, q4 * TOPK, E]), iota, ALU.is_equal), t, Q)
                        yield
                        t = dve.put(lambda e, js=js: e.tensor_reduce(
                            chosen[:, js, :], onehot[:, :, :].rearrange("p (j k) e -> p j e k", k=TOPK), AX.X,
                            ALU.add), t, Q)
                        yield
                    st["t"] = dve.put(lambda e: e.tensor_copy(chosen_bf[:, :, :], chosen[:, :, :]), t, Q)

                def count():
                    m, ps, free = take_misc()
                    before = ps[:, :].rearrange("p (j e) -> p j e", e=E)
                    pe.put(lambda e: e.matmul(before, strict_bf[:, :], chosen_bf[:, :, :], start=True, stop=False,
                                              skip_group_check=True), st["t"] + free + tab_ready + ones_ready)
                    for j in range(TILES - 1):
                        mm = pe.put(lambda e, j=j: e.matmul(
                            before[:, j + 1:TILES, :], ones_bf[:, :],
                            chosen_bf[:, j:j + 1, :].to_broadcast([P, TILES - 1 - j, E]), start=False,
                            stop=(j == TILES - 2), skip_group_check=True), (), s_misc if j == TILES - 2 else None)
                    t = dve.put(lambda e: e.tensor_tensor(
                        slot_of[:, :, :], before, taken[:, :].unsqueeze(1).to_broadcast([P, TILES, E]), ALU.add),
                        mm + ones_ready, Q)
                    misc["free"][m] = t
                    m, ps2, free = take_misc()
                    for j in range(TILES):
                        mm = pe.put(lambda e, j=j: e.matmul(ps2[:, 0:E], ones_bf[:, :], chosen_bf[:, j, :],
                                                            start=(j == 0), stop=(j == TILES - 1)),
                                    free, s_misc if j == TILES - 1 else None)
                    dve.put(lambda e: e.tensor_tensor(taken[:, :], ps2[:, 0:E], taken[:, :], ALU.add), mm + t, Q)
                    misc["free"][m] = [(Q, Q.count)]
                    yield
                    t = dve.put(lambda e: e.tensor_scalar(over[:, :, :], slot_of[:, :, :], float(CAP), float(NOWHERE),
                                                          ALU.is_ge, ALU.mult), t, Q)
                    t = dve.put(lambda e: e.tensor_tensor(
                        slot_of[:, :, :], slot_of[:, :, :],
                        tab[:, K_BASE:K_BASE + E].unsqueeze(1).to_broadcast([P, TILES, E]), ALU.add), t, Q)
                    st["t"] = dve.put(lambda e: e.tensor_tensor(slot_of[:, :, :], slot_of[:, :, :], over[:, :, :],
                                                                ALU.add), t, Q)

                def expert_weights():
                    t = dve.put(lambda e: e.tensor_tensor(scores[:, :, :], scores[:, :, :], chosen[:, :, :], ALU.mult),
                                st["t"], Q)
                    t = dve.put(lambda e: e.tensor_reduce(top_sum[:, :], scores[:, :, :], AX.X, ALU.add), t, Q)
                    t = dve.put(lambda e: e.tensor_scalar(top_sum[:, :], top_sum[:, :], TOPK_EPS, None, ALU.add), t, Q)
                    t = dve.put(lambda e: e.reciprocal(top_rec[:, :], top_sum[:, :]), t, Q)
                    yield
                    st["w"] = dve.put(lambda e: e.tensor_tensor(
                        rows[:, :, C:C + E], scores[:, :, :], top_rec[:, :].unsqueeze(2).to_broadcast([P, TILES, E]),
                        ALU.mult), t + st["rows_free"], Q)

                def dispatch():
                    t = st["t"]
                    q4 = TILES // 4
                    iota = tab[:, K_IOTA:K_IOTA + E].unsqueeze(1).to_broadcast([P, q4 * TOPK, E])
                    for q in range(4):
                        js = slice(q * q4, (q + 1) * q4)
                        t = dve.put(lambda e, js=js: e.tensor_tensor(
                            onehot[:, :, :], chosen_at[:, js, :].rearrange("p j k -> p (j k)").unsqueeze(2)
                            .to_broadcast([P, q4 * TOPK, E]), iota, ALU.is_equal), t, Q)
                        yield
                        for jj in range(q4):
                            t2 = dve.put(lambda e, j=q * q4 + jj, jj=jj: e.tensor_tensor(
                                onehot[:, jj * TOPK:(jj + 1) * TOPK, :], onehot[:, jj * TOPK:(jj + 1) * TOPK, :],
                                slot_of[:, j:j + 1, :].to_broadcast([P, TOPK, E]), ALU.mult), t, Q)
                        t = dve.put(lambda e, js=js: e.tensor_reduce(
                            slot_f[:, js, :].rearrange("p j k -> p (j k)"), onehot[:, :, :], AX.X, ALU.add), t2, Q)
                        st["slot"] = dve.put(lambda e, js=js: e.tensor_copy(slot_u[:, js, :], slot_f[:, js, :]),
                                             t + st["rows_free"], Q)
                        for jj in range(q4):
                            scatter(q * q4 + jj)
                        yield

                def scatter(j):
                    for k in range(TOPK):
                        t = pool.put(lambda e, k=k: e.indirect_dma_start(
                            out=slots, out_offset=bass.IndirectOffsetOnAxis(ap=slot_u[:, j, k:k + 1], axis=0),
                            in_=rows[:, j, :], in_offset=None, bounds_check=E * CAP - 1, oob_is_err=False),
                            st["slot"] + st["w"] + st["token"] + [(s_slots0, s_slots0.count)] + ones_ready, s_scatter)
                    tok["scatter"] = t
                    tok["rows_read"] = t + [(s_x1_out, s_x1_out.count)]

                for stage in (layer_norm, turn_x1, logits, top, expert_weights, count, dispatch):
                    yield from stage()
                    yield

            AHEAD = 3
            UNITS = len(units) // (B * H)
            MUST_AT, BACKGROUND_AT = (0, 2, 5, 8, 10, 11, 12, 14, 15, 16), range(1, UNITS)
            GATE_STEPS = 5
            ARGS_AT = {2: 2, 6: 3, 9: NG, 17: NG + 1}
            PREPARE_AT = 17
            LOAD_AT = {7: 0, 8: 1, 10: 2, 18: 3}
            LATE = ((3, 2), (2, 2), (2, 6), (2, 2))
            prepare_batch(0)
            load_qkv_weights(0)
            load_out_weights(0)
            gate_steps = gates(0)
            next(gate_steps)
            next(gate_steps)
            tasks = qkv_tasks(0)
            for task in tasks[:5]:
                task()
            for step in gate_steps:
                pass
            load_decay(0, 0)
            load_decay(0, 1)
            for task in tasks[5:]:
                task()
            for k in range(2):
                decay_args(0, k)
                decay_matrices(0, k)
                load_decay(0, k + 2)
            load_qkv_weights(1)
            late = []
            background = iter(())
            must = []

            def run_late(u):
                for item in sorted((x_ for x_ in late if x_[0] <= u), key=lambda x_: x_[1]):
                    late.remove(item)
                    _, what, n_, g_, ready = item
                    if what == "turn":
                        late.append((u + LATE[g_][1], "project", n_, g_, turn(n_, g_, ready)))
                    else:
                        project(n_, g_, ready)

            catch_up()
            for u in range(AHEAD):
                if u:
                    pair_a(u - 1)
                square(u, score_tile(u))
            for u, (n, g, s) in enumerate(units):
                at = u % UNITS
                catch_up()
                if u + AHEAD - 1 < len(units):
                    pair_a(u + AHEAD - 1)
                if s == 0:
                    if g == 0:
                        if n < H - 1:
                            fill_dram(n, H - 1)
                        if n + 1 < B * H:
                            if (n + 1) % H == 0:
                                gate_steps = gates((n + 1) // H)
                                must += [lambda: next(gate_steps)] * GATE_STEPS
                            must += qkv_tasks(n + 1)
                if u + AHEAD < len(units):
                    if units[u + AHEAD][0] != n:
                        while must:
                            must.pop(0)()
                    square(u + AHEAD, score_tile(u + AHEAD))
                value_product(u)
                if at - 1 in ARGS_AT:
                    n1, g1 = n + ARGS_AT[at - 1] // NG, ARGS_AT[at - 1] % NG
                    if n1 < B * H:
                        decay_matrices(n1, g1)
                if s >= 2 * g:
                    merge(n, g, s - 2 * g)
                if s == 2 * g + 1:
                    late.append((u + LATE[g][0], "turn", n, g, normalise(n, g)))
                if at in ARGS_AT:
                    n1, g1 = n + ARGS_AT[at] // NG, ARGS_AT[at] % NG
                    if n1 < B * H:
                        decay_args(n1, g1)
                if at in LOAD_AT and n + 1 < B * H:
                    load_decay(n + 1, LOAD_AT[at])
                run_late(u)
                if must and (at in MUST_AT or len(must) > sum(x_ > at for x_ in MUST_AT)):
                    must.pop(0)()
                elif at in BACKGROUND_AT:
                    next(background, None)
                if (g, s) == (1, 1):
                    assert not [x_ for x_ in late if x_[2] < n]
                    if n + 1 < B * H:
                        load_out_weights(n + 1)
                    if n + 2 < B * H:
                        load_qkv_weights(n + 2)
                    if n % H == 0 and n:
                        assert next(background, None) is None
                        background = route(n // H - 1)
                if at == PREPARE_AT and (n + 2) % H == 0 and n + 2 < B * H:
                    prepare_batch((n + 2) // H)
                if (g, s) == (NG - 1, 2 * NG - 1):
                    tok["heads", n // H] = av_done[u] + tok["num"]
            u = len(units)
            while late:
                catch_up()
                run_late(u)
                u += 1
            catch_up()
            assert next(background, None) is None
            last_route = route(B - 1)
            att_done = (tok["proj", B * H - 1] + [(s, s.count) for s in (
                s_acc, s_yt_hi, s_a_hi, s_a_lo, s_y, s_w_split, s_wc_split, s_mask_act, s_num, s_off, s_av, s_acc0,
                s_gate_act, s_gate_dve, s_qkv_lo, s_slots0, s_decay_out)])

        with ExitStack() as ffn:
            WS, XS, YS, HS, XE = 4, 5, 3, 4, 4
            w_raw_f = [sb(ffn, f"w_raw_f{i}", [P, WEIGHTS]) for i in range(2)]
            wf_hi = [sb(ffn, f"wf_hi{i}", [P, WEIGHTS], F32R) for i in range(WS)]
            wf_lo = [sb(ffn, f"wf_lo{i}", [P, WEIGHTS], F32R) for i in range(WS)]
            gate_up_w = lambda a: a[:, 0:CC * GU].rearrange("p (c f) -> p c f", c=CC)
            down_w = lambda a: a[:, CC * GU:].rearrange("p (k m) -> p k m", k=2)
            xr = [sb(ffn, f"xr{i}", [P, MT, ROW]) for i in range(XS)]
            xe_hi = [sb(ffn, f"xe_hi{i}", [P, CC, MAIN], F32R) for i in range(XE)]
            xe_lo = [sb(ffn, f"xe_lo{i}", [P, CC, MAIN], F32R) for i in range(XE)]
            silu_a = sb(ffn, "silu_a", [P, MAIN])
            silu_b = sb(ffn, "silu_b", [FB, MAIN])
            h_a = sb(ffn, "h_a", [P, MAIN])
            h_b = sb(ffn, "h_b", [FB, MAIN])
            ha_hi = [sb(ffn, f"ha_hi{i}", [P, MAIN], F32R) for i in range(HS)]
            ha_lo = [sb(ffn, f"ha_lo{i}", [P, MAIN], F32R) for i in range(HS)]
            hb = [sb(ffn, f"hb{i}", [KB, MAIN], F32R) for i in range(HS)]
            y_e = [sb(ffn, f"y_e{i}", [P, MT, C]) for i in range(YS)]

            c_raw = [signal(f"c_raw{i}", 16) for i in range(2)]
            c_zero, c_wh, c_wl = signal("c_zero"), signal("c_wh"), signal("c_wl")
            c_x = [signal(f"c_x{i}", 16) for i in range(XE)]
            c_r = [signal(f"c_r{i}", 16) for i in range(XS)]
            c_xh, c_xl, c_t = signal("c_xh"), signal("c_xl"), signal("c_t")
            c_gu, c_silu, c_h, c_hh, c_hl, c_dn, c_y = (signal(k) for k in (
                "c_gu", "c_silu", "c_h", "c_hh", "c_hl", "c_dn", "c_y"))
            c_store = [signal(f"c_store{i}", 16) for i in range(YS)]
            c_over = signal("c_over")
            c_yd, c_count = signal("c_yd"), signal("c_count")
            c_add = [signal(f"c_add{i}", 16) for i in range(2)]

            zero = att_done
            for i in range(HS):
                zero = pool.put(lambda e, i=i: e.memset(f32(hb[i][:, :]), 0.0), att_done, c_zero)
            use = {}
            job = {}

            slot_w = lambda x_id: x_id % WS if x_id < E else WS - 2 + x_id - E

            def weights_load(x_id):
                i = job["raw", x_id] = use["raw_n"] = (use.get("raw_n", -1) + 1) % 2
                job["raw_in", x_id] = sp.put(lambda e: e.dma_start(w_raw_f[i][:, :], wffn[x_id]),
                                             att_done + use.get(("raw", i), []), c_raw[i])

            def weights_split(x_id):
                i, w = job["raw", x_id], slot_w(x_id)
                free = use.get(("w_read", w), []) + att_done
                t = act.put(lambda e: e.activation(wf_hi[w][:, :], w_raw_f[i][:, :], ACT.Copy),
                            job["raw_in", x_id] + free, c_wh)

                def low():
                    use["raw", i] = use["w", w] = dve.put(lambda e: e.tensor_tensor(
                        wf_lo[w][:, :], w_raw_f[i][:, :], f32(wf_hi[w][:, :]), ALU.subtract), t + free, c_wl)
                return low

            gu_free = [[], []]

            def gate_up(k, w, x_hi, x_lo, width, ready):
                b0 = 3 * (k % 2)
                g_hi, g_lo = gate_up_w(wf_hi[w]), gate_up_w(wf_lo[w])
                mms = []
                for n, cols in enumerate((slice(0, P), slice(P, 2 * P), slice(2 * P, GU))):
                    m = cols.stop - cols.start
                    mms.append(product(bank[b0 + n][0:m, 0:width], [(g_hi[:, c, cols], g_lo[:, c, cols], x_hi[:, c, :],
                                                                     x_lo[:, c, :]) for c in range(CC)],
                                       ready + use["w", w] + gu_free[k % 2], c_gu))
                return mms

            def hidden(k, width, mms):
                b0, i = 3 * (k % 2), k % HS
                free = use.get(("h", i), [])
                ga, ua = bank[b0][:, 0:width], bank[b0 + 1][:, 0:width]
                gb, ub = bank[b0 + 2][0:FB, 0:width], bank[b0 + 2][FBO:KB, 0:width]
                sa, ha = silu_a[:, 0:width], h_a[:, 0:width]
                sb_, hb32 = silu_b[:, 0:width], h_b[:, 0:width]
                t = act.put(lambda e: e.activation(sa, ga, ACT.Silu), mms[0] + use.get("silu_a_read", []), c_silu)
                yield
                d = dve.put(lambda e: e.tensor_tensor(ha, ua, sa, ALU.mult), mms[1] + t + use.get("h_a_read", []), c_h)
                use["silu_a_read"] = d
                t2 = act.put(lambda e: e.activation(ha_hi[i][:, 0:width], ha, ACT.Copy), d + free, c_hh)
                yield
                tb = act.put(lambda e: e.activation(sb_, gb, ACT.Silu), mms[2] + use.get("silu_b_read", []), c_silu)
                db = dve.put(lambda e: e.tensor_tensor(hb32, ub, sb_, ALU.mult), tb + use.get("h_b_read", []), c_h)
                use["silu_b_read"] = db
                use["h_a_read"] = dve.put(lambda e: e.tensor_tensor(ha_lo[i][:, 0:width], ha, f32(ha_hi[i][:, 0:width]),
                                                                    ALU.subtract), t2 + d + free, c_hl)
                gu_free[k % 2] = t + d + tb + db
                yield
                tb2 = act.put(lambda e: e.activation(hb[i][0:FB, 0:width], hb32, ACT.Copy), db + free + zero, c_hh)
                use["h_b_read"] = dve.put(lambda e: e.tensor_tensor(hb[i][FBO:KB, 0:width], hb32, f32(hb[i][0:FB, 0:width]),
                                                                    ALU.subtract), tb2 + db + free, c_hl)
                job["h", k] = tb2 + use["h_a_read"] + use["h_b_read"]
                yield

            def down(steps, t0, dst, needs, first):
                mms = []
                for k, w in steps:
                    i, ts = k % HS, slice(t0, t0 + P)
                    d_hi, d_lo = down_w(wf_hi[w]), down_w(wf_lo[w])
                    mms += [(ha_hi[i][:, ts], d_hi[:, 0, :]), (ha_hi[i][:, ts], d_lo[:, 0, :]),
                            (ha_lo[i][:, ts], d_hi[:, 0, :]),
                            (hb[i][:, ts], d_hi[0:KB, 1, :]), (hb[i][:, ts], d_lo[0:KB, 1, :])]
                for n, (a, b_) in enumerate(mms):
                    done = pe.put(lambda e, a=a, b_=b_, n=n: e.matmul(dst, a, b_, start=(first and n == 0),
                                                                      stop=(n == len(mms) - 1), skip_group_check=True),
                                  needs if n == 0 else (), c_dn if n == len(mms) - 1 else None)
                return done

            sh = (E, E + 1)
            k = 0
            M = N // MAIN

            def shared_load(m):
                i, r = m % XE, m % XS
                ms = slice(m * MAIN, (m + 1) * MAIN)
                stores = x1_stored[m * MAIN // T]
                need = stores + use.get(("xe", i), []) + att_done
                sp.put(lambda e: e.dma_start(f32(xe_hi[i][:, :, :]), x1t_dram[0, :, :, ms]), need, c_x[i])
                job["x", m] = sp.put(lambda e: e.dma_start(f32(xe_lo[i][:, :, :]), x1t_dram[1, :, :, ms]), (), c_x[i])
                job["r", m] = sp.put(lambda e: e.dma_start(
                    xr[r][:, :, 0:C], x1_dram[ms, :].rearrange("(j p) c -> p j c", p=P)), use.get(("xr", r), []), c_r[r])

            def shared_up(m):
                nonlocal k
                i = m % XE
                job["k", m] = k
                for w in sh:
                    mms = gate_up(k, slot_w(w), xe_hi[i][:, :, :], xe_lo[i][:, :, :], MAIN, job["x", m])
                    for step in hidden(k, MAIN, mms):
                        pass
                    k += 1
                use["xe", i] = [(c_gu, c_gu.count)]

            def shared_down(m):
                r, y, k0 = m % XS, m % YS, job["k", m]
                steps = [(k0, slot_w(sh[0])), (k0 + 1, slot_w(sh[1]))]
                for pair in range(MAIN // GROUP):
                    q, ps, free = take_misc()
                    for jj in range(2):
                        mm = down(steps, (2 * pair + jj) * P, ps[:, jj * C:(jj + 1) * C],
                                  job["h", k0] + job["h", k0 + 1] + free, jj == 0)
                    t = dve.put(lambda e, ps=ps, pair=pair: e.tensor_tensor(
                        y_e[y][:, 2 * pair:2 * pair + 2, :], ps[:, :].rearrange("p (j c) -> p j c", c=C),
                        xr[r][:, 2 * pair:2 * pair + 2, 0:C], ALU.add),
                        mm + job["r", m] + use.get(("y", y), []) + att_done, c_yd)
                    misc["free"][q] = t
                for kk, w in steps:
                    use["h", kk % HS] = mm
                    use["w_read", w] = mm
                use["xr", r] = t
                use["y", y] = sp.put(lambda e: e.dma_start(y_part[0][m * MAIN:(m + 1) * MAIN, :].rearrange(
                    "(j p) c -> p j c", p=P), y_e[y][:, :, :]), t, c_store[y])

            def expert_load(x_id, r, first, tiles):
                s0 = x_id * CAP + first * P
                job["xr", r] = sp.put(lambda e: e.dma_start(
                    xr[r][:, 0:tiles, :], slots[s0:s0 + tiles * P, :].rearrange("(j p) c -> p j c", p=P)),
                    tok["scatter"] + use.get(("xr", r), []), c_r[r])

            def expert_turn(r, i, tiles):
                for pair in range(tiles // 2):
                    q, ps, free = take_misc()
                    for jj in range(2):
                        for c in range(CC):
                            mm = pe.put(lambda e, jj=jj, c=c, ps=ps, pair=pair: e.transpose(
                                ps[:, c * GROUP + jj * P:c * GROUP + (jj + 1) * P],
                                xr[r][:, 2 * pair + jj, c * P:(c + 1) * P], ident),
                                job["xr", r] + free, c_t if (jj, c) == (1, CC - 1) else None)
                    src = ps[:, :].rearrange("p (c t) -> p c t", c=CC)
                    ts = slice(pair * GROUP, (pair + 1) * GROUP)
                    free = use.get(("xe", i), [])
                    t = act.put(lambda e, src=src, ts=ts: e.activation(xe_hi[i][:, :, ts], src, ACT.Copy), mm + free, c_xh)
                    t2 = dve.put(lambda e, src=src, ts=ts: e.tensor_tensor(xe_lo[i][:, :, ts], src, f32(xe_hi[i][:, :, ts]),
                                                                           ALU.subtract), mm + t + free, c_xl)
                    misc["free"][q] = t + t2
                job["xe", i] = t + t2

            def expert_down(x_id, kk, r, y, tiles, tells):
                part = x_id % 2
                for j in range(tiles):
                    q, ps, free = take_misc()
                    mm = down([(kk, slot_w(x_id))], j * P, ps[:, 0:C], job["h", kk] + free, True)
                    t = act.put(lambda e, j=j, ps=ps: e.activation(y_e[y][:, j, :], ps[:, 0:C], ACT.Copy,
                                                                   scale=xr[r][:, j, C + x_id:C + x_id + 1]),
                                mm + use.get(("y", y), []), c_y)
                    misc["free"][q] = t
                    added = pool.put(lambda e, j=j: e.indirect_dma_start(
                        out=y_part[part], out_offset=bass.IndirectOffsetOnAxis(
                            ap=xr[r][:, j, TOKEN_COL:TOKEN_COL + 1].bitcast(U32), axis=0),
                        in_=y_e[y][:, j, :], in_offset=None, bounds_check=N + CAP - 1, oob_is_err=True,
                        compute_op=ALU.add), t + [(q_, q_.count) for q_ in c_store] + use.get(("added", part), []), tells)
                use["h", kk % HS] = mm
                use["w_read", slot_w(x_id)] = mm
                use["added", part] = use["y", y] = use["xr", r] = added

            for x_id in sh:
                weights_load(x_id)
            for m in range(XE):
                shared_load(m)
            for x_id in sh:
                weights_split(x_id)()

            def route_some(count):
                for _ in range(count):
                    next(last_route, None)

            route_some(10)
            shared_up(0)
            for m in range(M):
                if m + 1 < M:
                    shared_up(m + 1)
                route_some(7)
                shared_down(m)
                route_some(6)
                if m + XE < M:
                    shared_load(m + XE)
                if m < 2:
                    weights_load(m)
                if m in (2, 3):
                    weights_split(m - 2)()
            for step in last_route:
                pass
            dve.put(lambda e: e.tensor_copy(counts[:, :], taken[0:1, :]), [(s_route, s_route.count)], c_count)
            t = dve.put(lambda e: e.tensor_reduce(most_f[:, :], taken[0:1, :].rearrange("p (g x) -> p g x", x=OVER_GROUP),
                                                  AX.X, ALU.max), (), c_count)
            counted = dve.put(lambda e: e.tensor_copy(most[:, :], most_f[:, :]), t, c_count)

            for x_id in range(2):
                expert_load(x_id, x_id % XS, 0, MT)
            weights_load(2)
            expert_turn(0, 0, MT)
            step = {}
            for x_id in range(E):
                if x_id + 2 < E:
                    expert_load(x_id + 2, (x_id + 2) % XS, 0, MT)
                if x_id + 3 < E:
                    weights_load(x_id + 3)
                if x_id + 1 < E:
                    expert_turn((x_id + 1) % XS, (x_id + 1) % 2, MT)
                i = x_id % 2
                step[x_id] = k
                mms = gate_up(k, slot_w(x_id), xe_hi[i][:, :, :], xe_lo[i][:, :, :], MAIN, job["xe", i])
                use["xe", i] = mms[2]
                h_steps = hidden(k, MAIN, mms)
                next(h_steps)
                if x_id + 2 < E:
                    split_lo = weights_split(x_id + 2)
                next(h_steps)
                if x_id + 2 < E:
                    split_lo()
                next(h_steps)
                if x_id:
                    expert_down(x_id - 1, k - 1, (x_id - 1) % XS, (x_id - 1) % YS, MT,
                                c_add[(x_id - 1) % 2])
                next(h_steps)
                k += 1
            expert_down(E - 1, k - 1, (E - 1) % XS, (E - 1) % YS, MT, c_add[(E - 1) % 2])

            engines = (pe, act, dve, pool, sp)
            over_added = [signal(f"over_added{x_id}", 16, once=True) for x_id in range(E)]
            tiles = CT - MT
            width = tiles * P

            def over_main(ap):
                return lambda e: e.value_load(ap, min_val=0, max_val=N) > MAIN

            def rows_are_added(parts):
                return pool.put(lambda e: e.memset(over_flag[:, :], 0.0), [t for p in parts for t in use["added", p]],
                                c_over)

            use["added", 0] = use["added", 1] = rows_are_added((0, 1))
            for i in range(YS):
                use["y", i] = use["added", 0]
            for i in range(XS):
                use["xr", i] = use["added", 0]
            for x_id in range(E):
                if x_id % OVER_GROUP == 0:
                    for q in engines:
                        q.begin_if()
                for q in engines:
                    q.begin_if()
                r, y = x_id % XS, x_id % YS
                expert_load(x_id, r, MT, tiles)
                weights_load(x_id)
                expert_turn(r, 0, tiles)
                weights_split(x_id)()
                mms = gate_up(k, slot_w(x_id), xe_hi[0][:, :, 0:width], xe_lo[0][:, :, 0:width], width, job["xe", 0])
                use["xe", 0] = mms[2]
                for step in hidden(k, width, mms):
                    pass
                expert_down(x_id, k, r, y, tiles, over_added[x_id])
                k += 1
                use["added", x_id % 2] = use["xr", r] = use["y", y] = rows_are_added((x_id % 2,))
                for q in engines:
                    q.end_if((), over_main(counts[0:1, x_id:x_id + 1]))
                if x_id % OVER_GROUP == OVER_GROUP - 1:
                    g = x_id // OVER_GROUP
                    for q in engines:
                        q.end_if(counted, over_main(most[0:1, g:g + 1]))

            DT = 4
            DS = 2 * TILES // DT
            part1 = y_e
            d_in = [signal(f"d_in{i}", 16) for i in range(DS)]
            d_sum, d_dve, d_act = signal("d_sum"), signal("d_dve"), signal("d_act")
            d_out = signal("d_out", 16)
            all_added = use["added", 0] + use["added", 1]

            def y_norm(n):
                i = n % DS
                js = slice(i % 2 * DT, (i % 2 + 1) * DT)
                y, p1 = acc[i // 2][:, js, :], part1[n % YS]
                ns = slice(n * DT * P, (n + 1) * DT * P)
                st_, mv_, sd, rs = stats[:, js, :], mv[:, js, :], std[:, js], rstd[:, js]
                sp.put(lambda e: e.dma_start(y, y_part[0][ns, :].rearrange("(j p) c -> p j c", p=P)),
                       all_added + tok["ln", B - 1] + tok["ln", B - 2] + tok.get(("out", n - DS), []), d_in[i])
                got = sp.put(lambda e: e.dma_start(p1[:, :, :], y_part[1][ns, :].rearrange("(j p) c -> p j c", p=P)),
                             tok.get(("sum", n - YS), []), d_in[i])
                t = tok["sum", n] = pool.put(lambda e: e.tensor_tensor(y, y, p1[:, :, :], ALU.add), got, d_sum)
                yield
                for j in range(DT):
                    dve.put(lambda e, j=j: e.bn_stats(st_[:, j, :], y[:, j, :]), t, d_dve)
                t = [(d_dve, d_dve.count)]
                for j in range(DT):
                    t2 = dve.put(lambda e, j=j: e.bn_aggr(mv_[:, j, :], st_[:, j, :]), t + tok.get(("norm", n - 2), []),
                                 d_dve)
                t = dve.put(lambda e: e.tensor_scalar(sd, mv_[:, :, 1], LN_EPS, None, ALU.add), t2, d_dve)
                t = act.put(lambda e: e.activation(sd, sd, ACT.Sqrt), t, d_act)
                yield
                t = dve.put(lambda e: e.reciprocal(rs, sd), t, d_dve)
                for j in range(DT):
                    t2 = dve.put(lambda e, j=j: e.tensor_scalar(y[:, j, :], y[:, j, :], mv_[:, j, 0:1], rs[:, j:j + 1],
                                                                ALU.subtract, ALU.mult), t, d_dve)
                tok["norm", n] = t2
                tok["out", n] = sp.put(lambda e: e.dma_start(out[ns, :].rearrange("(j p) c -> p j c", p=P), y), t2, d_out)
                yield

            n_steps = N // (DT * P)
            in_flight = [y_norm(n) for n in range(n_steps)]
            for n in range(n_steps + 3):
                for lag in (0, 2, 3):
                    if 0 <= n - lag < n_steps:
                        next(in_flight[n - lag])
            for s in (d_out, *c_store, s_x1_out, s_x1t_out, s_decay_out, s_slots0):
                sp.items.append(([(s.sem, s.count)], lambda e: None, None))
            for s in (s_scatter, *c_add, c_over):
                pool.items.append(([(s.sem, s.count)], lambda e: None, None))

        block = ctx.enter_context(nc.Block())
        block.sync(lambda e: Queue.run(e, sp.items))
        block.gpsimd(lambda e: Queue.run(e, pool.items))
        block.scalar(lambda e: Queue.run(e, act.items))
        block.vector(lambda e: Queue.run(e, dve.items))
        block.tensor(lambda e: Queue.run(e, pe.items))


def constants(np):
    t = np.zeros((P, K_END), np.float32)
    k, c = np.arange(P)[:, None], np.arange(P)[None, :]
    t[:, K_ID:K_ID + P] = k == c
    t[:, K_TRI:K_TRI + P] = k <= c
    t[:, K_STRICT:K_STRICT + P] = k < c
    t[:, K_MASK:K_MASK + P] = np.where(k <= c, 0.0, NEG)
    t[:, K_BASE:K_BASE + E] = np.arange(E) * CAP
    t[:, K_IOTA:K_IOTA + E] = np.arange(E)
    return t


def kernel(**inputs):
    import numpy as np
    import concourse.bacc as bacc
    from concourse.bass_utils import run_bass_kernel_spmd as run

    get = lambda name: np.asarray(inputs[name])
    x = np.ascontiguousarray(get("L0_attn_hidden_states").reshape(N, C))
    chunks = lambda w: w.reshape(CC, P, -1).transpose(1, 0, 2)
    wq = chunks(get("L0_attn_Wq")).reshape(P, CC, H, R * D)
    wk = chunks(get("L0_attn_Wk")).reshape(P, CC, H, D)
    wv = chunks(get("L0_attn_Wv")).reshape(P, CC, H, D)
    wc = get("L0_attn_Wc").reshape(H, R, D, C).transpose(0, 2, 1, 3).reshape(H, P, R * C)
    per_head = lambda w: w.transpose(2, 0, 1, 3).reshape(H, P, -1)
    wall = np.concatenate([per_head(wq), per_head(wk), per_head(wv), wc], axis=2)
    gate = np.concatenate([get("L0_ffn_w_gate"), get("L0_ffn_sh_gate").reshape(FS // F, F, C)])
    up = np.concatenate([get("L0_ffn_w_up"), get("L0_ffn_sh_up").reshape(FS // F, F, C)])
    wffn = np.zeros((NX, P, WEIGHTS), gate.dtype)
    gu = wffn[:, :, 0:CC * GU].reshape(NX, P, CC, GU)
    for o, block in ((0, gate[:, 0:P]), (P, up[:, 0:P]), (2 * P, gate[:, P:]), (2 * P + FBO, up[:, P:])):
        gu[:, :, :, o:o + block.shape[1]] = block.reshape(NX, -1, CC, P).transpose(0, 3, 2, 1)
    wffn[:, :, 0:CC * GU] = gu.reshape(NX, P, CC * GU)
    dn = np.concatenate([get("L0_ffn_w_down").transpose(0, 2, 1), get("L0_ffn_sh_down").T.reshape(FS // F, F, C)])
    wffn[:, :, CC * GU:CC * GU + C] = dn[:, 0:P]
    for o in (0, FBO):
        wffn[:, o:o + FB, CC * GU + C:] = dn[:, P:]
    arrays = {
        "xT": x.T.reshape(CC, P, N).transpose(1, 0, 2), "x": x, "wall": wall, "wg": chunks(get("L0_attn_Wg")),
        "gw": chunks(get("L0_ffn_gate_w").T), "bc": get("L0_attn_bc"), "wffn": wffn, "table": constants(np),
    }
    arrays = {f"in_{k}": np.ascontiguousarray(v) for k, v in arrays.items()}
    nc = bacc.Bacc("TRN2", target_bir_lowering=False, num_devices=1)
    aps = [nc.dram_tensor(k, v.shape, mybir.dt.from_np(v.dtype), kind="ExternalInput").ap() for k, v in arrays.items()]
    out = nc.dram_tensor("out_rows", (N, C), F32, kind="ExternalOutput").ap()
    build(nc, *aps, out)
    result = run(nc, [arrays], core_ids=[0])
    return result.results[0]["out_rows"].reshape(B, T, C)
```
